# Optimizing a Trainium2 kernel written in Bass

```python
import numpy as np
import jax
import jax.numpy as jnp

def _softmax(x, axis=-1):
    return jax.nn.softmax(x, axis=axis)

def _gelu(x):
    return jax.nn.gelu(x, approximate=True)

def _silu(x):
    return jax.nn.silu(x)

def _sigmoid(x):
    return jax.nn.sigmoid(x)

def _layernorm(x, axis=-1, eps=1e-05):
    m = jnp.mean(x, axis=axis, keepdims=True)
    v = jnp.var(x, axis=axis, keepdims=True)
    return (x - m) / jnp.sqrt(v + eps)

def _scatter_add(tgt, idx, src, axis=0):
    return tgt.at[idx].add(src)

def _segment_sum(src, seg, n):
    return jax.ops.segment_sum(src, seg, n)
kernel_name = 'mk_prb_d1_jaxref_r8_9a3f7e'

def setup_inputs(seed: int=0):
    np.random.seed(seed)
    _w = jnp.asarray

    def _L0_attn_setup():
        import jax, jax.numpy as jnp
        import numpy as np
        B, S, E, H = (4, 256, 128, 16)
        D = E // H

        def _split_heads(x):
            b, s, _ = x.shape
            return x.reshape(b, s, H, D).transpose(0, 2, 1, 3)
        key = jax.random.key(seed)
        ks = jax.random.split(key, 6)
        scale = 1.0 / np.sqrt(E)
        return {'inputs': jax.random.normal(ks[0], (B, S, E), dtype=jnp.float32), 'Wq': jax.random.normal(ks[1], (E, E), dtype=jnp.float32) * scale, 'bq': jnp.zeros((E,), dtype=jnp.float32), 'Wk': jax.random.normal(ks[2], (E, E), dtype=jnp.float32) * scale, 'bk': jnp.zeros((E,), dtype=jnp.float32), 'Wv': jax.random.normal(ks[3], (E, E), dtype=jnp.float32) * scale, 'bv': jnp.zeros((E,), dtype=jnp.float32), 'Wo': jax.random.normal(ks[4], (E, E), dtype=jnp.float32) * scale, 'bo': jnp.zeros((E,), dtype=jnp.float32)}
    _L0_attn_in = _L0_attn_setup()

    def _L0_ffn_setup():
        import jax, jax.numpy as jnp
        import numpy as np
        TOP_K = 2
        key = jax.random.key(seed)
        k0, k1, k2, k3, k4 = jax.random.split(key, 5)
        B, S, D, H, E = (4, 256, 128, 256, 8)
        x = jax.random.normal(k0, (B, S, D), dtype=jnp.float32)
        router_w = jax.random.normal(k1, (E, D), dtype=jnp.float32) * D ** (-0.5)
        w_gate = jax.random.normal(k2, (E, D, H), dtype=jnp.float32) * D ** (-0.5)
        w_up = jax.random.normal(k3, (E, D, H), dtype=jnp.float32) * D ** (-0.5)
        w_down = jax.random.normal(k4, (E, H, D), dtype=jnp.float32) * H ** (-0.5)
        return {'x': x, 'router_w': router_w, 'w_gate': w_gate, 'w_up': w_up, 'w_down': w_down}
    _L0_ffn_in = _L0_ffn_setup()
    _d = {'L0_attn_inputs': _L0_attn_in['inputs'], 'L0_attn_Wq': _L0_attn_in['Wq'], 'L0_attn_bq': _L0_attn_in['bq'], 'L0_attn_Wk': _L0_attn_in['Wk'], 'L0_attn_bk': _L0_attn_in['bk'], 'L0_attn_Wv': _L0_attn_in['Wv'], 'L0_attn_bv': _L0_attn_in['bv'], 'L0_attn_Wo': _L0_attn_in['Wo'], 'L0_attn_bo': _L0_attn_in['bo'], 'L0_ffn_router_w': _L0_ffn_in['router_w'], 'L0_ffn_w_gate': _L0_ffn_in['w_gate'], 'L0_ffn_w_up': _L0_ffn_in['w_up'], 'L0_ffn_w_down': _L0_ffn_in['w_down']}
    _x0 = _d['L0_attn_inputs']
    _d['L0_attn_inputs'] = jax.random.normal(jax.random.fold_in(jax.random.key(seed), 1), (4, 1024, 128), dtype=_x0.dtype)
    del _x0
    return _d

def reference(L0_attn_inputs, L0_attn_Wq, L0_attn_bq, L0_attn_Wk, L0_attn_bk, L0_attn_Wv, L0_attn_bv, L0_attn_Wo, L0_attn_bo, L0_ffn_router_w, L0_ffn_w_gate, L0_ffn_w_up, L0_ffn_w_down):

    def _L0_attn_ref(inputs, Wq, bq, Wk, bk, Wv, bv, Wo, bo):
        import jax, jax.numpy as jnp
        import numpy as np
        B, S, E, H = (4, 256, 128, 16)
        D = E // H

        def _split_heads(x):
            b, s, _ = x.shape
            return x.reshape(b, s, H, D).transpose(0, 2, 1, 3)
        q = _split_heads(inputs @ Wq + bq)
        k = _split_heads(inputs @ Wk + bk)
        v = _split_heads(inputs @ Wv + bv)
        inv_sqrt_d = jnp.float32(1.0) / jnp.sqrt(jnp.float32(D))
        scores = jnp.einsum('bhqd,bhkd->bhqk', q, k) * inv_sqrt_d
        weights = jax.nn.softmax(scores, axis=-1)
        attn = jnp.einsum('bhqk,bhkd->bhqd', weights, v)
        attn = attn.transpose(0, 2, 1, 3).reshape(inputs.shape[0], -1, E)
        return attn @ Wo + bo

    def _L0_ffn_ref(x, router_w, w_gate, w_up, w_down):
        import jax, jax.numpy as jnp
        import numpy as np
        TOP_K = 2
        B, S, D = x.shape
        E = router_w.shape[0]
        xt = x.reshape(-1, D)
        logits = xt @ router_w.T
        topk_vals, topk_idx = jax.lax.top_k(logits, TOP_K)
        g = jax.nn.sigmoid(topk_vals)
        g = g / (g.sum(axis=-1, keepdims=True) + 1e-10)
        out = jnp.zeros_like(xt)
        for e in range(E):
            ge = jnp.sum(jnp.where(topk_idx == e, g, jnp.zeros_like(g)), axis=-1)
            h = jax.nn.silu(xt @ w_gate[e]) * (xt @ w_up[e])
            out = out + ge[:, None] * (h @ w_down[e])
        return out.reshape(B, S, D)
    x = L0_attn_inputs
    xn = _layernorm(x, axis=-1)
    x = x + _L0_attn_ref(xn, L0_attn_Wq, L0_attn_bq, L0_attn_Wk, L0_attn_bk, L0_attn_Wv, L0_attn_bv, L0_attn_Wo, L0_attn_bo) + _L0_ffn_ref(xn, L0_ffn_router_w, L0_ffn_w_gate, L0_ffn_w_up, L0_ffn_w_down)
    return x

_drawn_inputs = setup_inputs


def setup_inputs(seed=0):
    import zlib

    import numpy as np

    out = dict(_drawn_inputs(seed))
    spreads = {'L0_attn_bq': (0.0, 0.8),
     'L0_attn_bk': (0.0, 0.8),
     'L0_attn_bv': (0.0, 0.1),
     'L0_attn_bo': (0.0, 0.1)}
    factors = {}
    for name, (base, spread) in spreads.items():
        noise = np.random.default_rng([zlib.crc32(name.encode()), seed]).standard_normal(out[name].shape)
        drawn = base * np.exp(spread * noise) if base else spread * noise
        out[name] = jnp.asarray(drawn.astype(out[name].dtype))
    for name, factor in factors.items():
        out[name] = (out[name] * factor).astype(out[name].dtype)
    return out
```

```python
from contextlib import ExitStack

import numpy as np
import concourse.bass as bass
from concourse import mybir

F32 = mybir.dt.float32
BF16 = mybir.dt.bfloat16
ALU = mybir.AluOpType
ACT = mybir.ActivationFunctionType
AX = mybir.AxisListType

P = 128
B, S, E = 4, 1024, 128
H = 16
D = E // H
NE = 8
F = 256
T = B * S
NT = T // P
CH = 512
NC = T // CH
TPC = CH // P
HG = 4
NG = B * H // HG
NH = 2 * NG
KT = S // P
PARTS = 3
ROWS = PARTS * PARTS * D
SHIFT = 96
KX = SHIFT
KS = SHIFT + PARTS
NBUF = 3
SCALE = float(np.float32(1.0) / np.sqrt(np.float32(D)))
EPS = 1e-5
BIG = 1.7e38
LOADS = 16 * (PARTS + PARTS * PARTS)


def build(nc, x, Wq, bq, Wk, bk, Wv, bv, Wo, bo, router_w, w_gate, w_up, w_down, out):
    ctx = ExitStack()
    with ctx:
        ctx.enter_context(nc.allow_non_contiguous_dma(reason="bias columns"))

        def sb(name, shape, dt=F32):
            return ctx.enter_context(nc.sbuf_tensor(name, shape, dt))

        def sem(name):
            return ctx.enter_context(nc.semaphore(name))

        def dram(name, shape, dt):
            return nc.dram_tensor(name, shape, dt).ap()

        parts_dram = [dram(f"{z}_parts", [B, HG, 2, PARTS, D * HG, CH], BF16) for z in "qk"]
        gates_dram = dram("gates", [NE, T], F32)
        shift_dram = dram("shift", [2, PARTS, HG * TPC, P], BF16)

        x_ffn = sb("x_ffn", [P, T])
        x_all = x_ffn[:, :].rearrange("p (n e) -> p n e", e=E)
        xnT_attn = sb("xnT_attn", [P, T])
        attn_all = xnT_attn[:, :].rearrange("p (n q c) -> p n q c", n=NH, q=TPC)
        v_all = sb("v_all", [P, B, HG, KT, HG * D])
        w_gu = sb("w_gu", [P, 2, NE, F])
        probs = w_gu[:, :, :, :].rearrange("p a b c -> p (a b c)").rearrange("p (u h q) -> p u h q", u=2, h=HG)
        w_dn = sb("w_dn", [P, NE, F // P, E])
        wq_in, wk_in, wv, wo = (sb(n, [P, E]) for n in ("wq_in", "wk_in", "wv", "wo"))
        wqk = sb("wqk", [P, 2, E])
        bqk = sb("bqk", [P, 2])
        bq_in = sb("bq_in", [P, 1])
        bo_col = sb("bo_col", [P, 1])
        bv_row = sb("bv_row", [P, E])
        rw_in = sb("rw_in", [NE, E])
        rwT = sb("rwT", [P, NE])
        ident = sb("ident", [P, P])
        rank = sb("rank", [P, NE])
        zero = sb("zero", [P, 1])
        stats = sb("stats", [P, NT, 6])
        mom = sb("mom", [P, 5, NT])
        xn = sb("xn", [P, 2, TPC, E])
        xnT_st = sb("xnT_st", [P, 2, CH])
        lg = sb("lg", [P, NT, NE])
        gm = sb("gm", [P, 8, 2, NT])
        gate_en = sb("gate_en", [P, NE, NT])
        gate_T = sb("gate_T", [P, 2, P])
        gate_bc = sb("gate_bc", [P, 4, 2, CH])
        silu = sb("silu", [P, 2, CH])
        hu = sb("hu", [P, 2, CH])
        hid = sb("hid", [P, 4, CH])
        gt = hid[:, :, :].rearrange("p a t -> p (a t)")[:, 0:6 * NT * NE].rearrange("p (k n e) -> p k n e", k=6, e=NE)
        qk_f = sb("qk_f", [P, 2, CH])
        qk_r = sb("qk_r", [P, 2, CH])
        qk_p = sb("qk_p", [P, 2, 2, PARTS, CH], BF16)
        qk_buf = sb("qk_buf", [P, NBUF, 2, 2, HG, CH], BF16)
        q_sb = [qk_buf[:, s, 0] for s in range(NBUF)]
        k_sb = [qk_buf[:, s, 1] for s in range(NBUF)]
        vx = [sb(f"vx{s}", [P, KT, HG, 32]) for s in range(NBUF)]
        mneg = sb("mneg", [P, 2, HG * TPC])
        m_parts = sb("m_parts", [HG * TPC, 2, PARTS, P], BF16)
        m_rest = sb("m_rest", [HG * TPC, 2, P])
        oT = xn[:, :, :, :].rearrange("p s j e -> p s (j e)")
        recip = sb("recip", [P, 2, HG * TPC])
        late = [qk_buf[:, s].rearrange("p z a h q -> p (z a h q)").bitcast(F32) for s in range(NBUF)]

        def late_tile(s, k):
            return late[s][:, k * CH:(k + 1) * CH]

        ps = ctx.enter_context(nc.psum_tensor("ps", [P, 8, CH], F32))

        x_t = x.rearrange("b (m p) e -> p (b m) e", p=P)
        out_c = out.rearrange("b (a q p) e -> (b a) p q e", a=2, q=TPC)
        x_c = x.rearrange("b (a q p) e -> (b a) p q e", a=2, q=TPC)

        def sems(name, n=2):
            return [sem(f"{name}{k}") for k in range(n)]

        x_in, proj_in, small_in, ffn_in = sems("x_in", 4), sem("proj_in"), sem("small_in"), sem("ffn_in")
        ident_step, const_step, stat_done, mom_step = (sem(n) for n in ("ident_step", "const_step", "stat_done", "mom_step"))
        var_ready, std_ready, rw_T, rw_ready = (sem(n) for n in ("var_ready", "std_ready", "rw_T", "rw_ready"))
        xn_ready, xn_T, xnT_st_ready, xnT_ready = (sems(n) for n in ("xn_ready", "xn_T", "xnT_st_ready", "xnT_ready"))
        v_ps, v_ready = sems("v_ps"), sems("v_ready")
        gexp_in, gexp_out, gate_ready, gate_Tps = (sem(n) for n in ("gexp_in", "gexp_out", "gate_ready", "gate_Tps"))
        gate_Tsb, gate_stored, gate_in = sem("gate_Tsb"), sem("gate_stored"), sems("gate_in", 4)
        gu_ready, silu_ready, hu_ready = (sems(n) for n in ("gu_ready", "silu_ready", "hu_ready"))
        hid_ready, down_done, ffn_ready = sems("hid_ready", 4), sems("down_done", 4), sems("ffn_ready")
        qk_ps, qk_f_ready, parts_ready, split_step = sems("qk_ps"), sems("qk_f_ready"), sems("parts_ready"), sem("split_step")
        parts_stored, qk_in = sems("parts_stored"), sems("qk_in", NBUF)
        rows_const, vx_const, vx_ready = sem("rows_const"), sem("vx_const"), sem("vx_ready")
        scores_ready, exp_done, pv_done = sem("scores_ready"), sem("exp_done"), sem("pv_done")
        x_ready, max_done, m_T = (sem(n) for n in ("x_ready", "max_done", "m_T"))
        m_hi, m_read, m_mid, m_rest2, m_split = (sem(n) for n in ("m_hi", "m_read", "m_mid", "m_rest2", "m_split"))
        m_stored, m_in = sem("m_stored"), sem("m_in")
        o_out, o_T, recip_ready, attn_ready = (sem(n) for n in ("o_out", "o_T", "recip_ready", "attn_ready"))
        a_staged, a_T, a_sb, a_proj, y_T_in, y_T, y_ready = (sems(n) for n in (
            "a_staged", "a_T", "a_sb", "a_proj", "y_T_in", "y_T", "y_ready"))
        x2_in, y_out = sems("x2_in"), sems("y_out")

        def group(i, c):
            return 3 * i + c // 2

        def buf(c):
            return (c // 2) % NBUF

        def turn(i, c):
            return i + c // 2 // NBUF

        def over_halves(eng, step):
            for c in range(2):
                step(0, c, c)
            with eng.Fori(0, (NH - 8) // 6) as i:
                for c in range(2, 8):
                    step(i, c, None)
            for c in range(NH - 6, NH):
                step(0, c, c)

        block = ctx.enter_context(nc.Block())

        @block.sync
        def _(sp):
            for k in range(4):
                n = NT // 4
                sp.dma_start(x_all[:, k * n:(k + 1) * n, :], x_t[:, k * n:(k + 1) * n, :]).then_inc(x_in[k], 16)
            sp.dma_start(wv[:, :], Wv).then_inc(proj_in, 16)
            sp.dma_start(wq_in[:, :], Wq).then_inc(proj_in, 16)
            sp.dma_start(wk_in[:, :], Wk).then_inc(proj_in, 16)
            sp.dma_start(wo[:, :], Wo).then_inc(proj_in, 16)
            sp.dma_start(rw_in[:, :], router_w).then_inc(small_in, 16)
            sp.dma_start(bv_row[:, :], bv.rearrange("(a e) -> a e", a=1).broadcast_to([P, E])).then_inc(small_in, 16)
            sp.dma_start(bo_col[:, :], bo.rearrange("(e a) -> e a", a=1)).then_inc(small_in, 16)
            for g in range(HG):
                for col, b_dram in ((bq_in[:, 0:1], bq), (bqk[:, 1:2], bk)):
                    for d in range(D):
                        r = g * 32 + d * HG
                        src = b_dram.rearrange("(g h d a) -> g d h a", g=HG, h=HG, a=1)[g, d]
                        sp.dma_start(col[r:r + HG, :], src).then_inc(small_in, 16)
            sp.dma_start(w_gu[:, 0, :, :], w_gate.rearrange("e d f -> d e f")).then_inc(ffn_in, 16)
            sp.dma_start(w_gu[:, 1, :, :], w_up.rearrange("e d f -> d e f")).then_inc(ffn_in, 16)
            sp.dma_start(w_dn[:, :, :, :].rearrange("p e k d -> p (e k) d"),
                         w_down.rearrange("e (k p) d -> p (e k) d", p=P)).then_inc(ffn_in, 16)

            sp.wait_ge(gate_Tsb, 1)
            sp.dma_start(gates_dram.rearrange("(k e) (n t) -> (e n) k t", k=2, t=P), gate_T[:, :, :]).then_inc(gate_stored, 16)
            sp.wait_ge(gate_stored, 16)

            def load_gates(c, r):
                sp.dma_start(gate_bc[:, r, :, :],
                             gates_dram[2 * r:2 * r + 2, bass.ds(c * CH, CH)].rearrange("(a e) t -> a e t", a=1)
                             .broadcast_to([P, 2, CH])).then_inc(gate_in[r], 16)

            def serve_chunk(i, s, more):
                c = 2 * i + s
                if more:
                    for r in range(4):
                        sp.wait_ge(hid_ready[3], 4 * c + r + 1)
                        load_gates(c + 1, r)
                for z in range(2):
                    sp.wait_ge(parts_ready[z], c + 1)
                    for k in range(PARTS):
                        sp.dma_start(parts_dram[z][bass.ds(i, 1), :, s, k].rearrange("b g r t -> (b g) r t"),
                                     qk_p[:, s, z, k, :]).then_inc(parts_stored[s], 16)
            for r in range(4):
                load_gates(0, r)
            with sp.Fori(0, NC // 2 - 1) as i:
                for s in range(2):
                    serve_chunk(i, s, True)
            serve_chunk(NC // 2 - 1, 0, True)
            serve_chunk(NC // 2 - 1, 1, False)
            for s in range(2):
                sp.wait_ge(parts_stored[s], 16 * 2 * PARTS * (NC // 2))

            def load_group(g, s):
                k_src = parts_dram[1].rearrange("b g a k (d h) t -> (b g) (k d) a (h t)", h=HG)[bass.ds(g, 1)] \
                    .rearrange("g r a t -> (g r) a t")
                for copy in range(PARTS):
                    r = copy * PARTS * D
                    sp.dma_start(k_sb[s][r:r + PARTS * D].rearrange("r a h t -> r a (h t)"), k_src).then_inc(qk_in[s], 16)
                for part in range(PARTS):
                    q_src = parts_dram[0].rearrange("b g a k (d h) t -> (b g) k d a (h t)", h=HG)[bass.ds(g, 1), part] \
                        .rearrange("g r a t -> (g r) a t")
                    for copy in range(PARTS):
                        r = (part * PARTS + copy) * D
                        sp.dma_start(q_sb[s][r:r + D].rearrange("r a h t -> r a (h t)"), q_src).then_inc(qk_in[s], 16)

            sp.wait_ge(rows_const, 4 * NBUF)
            for g in range(NBUF):
                load_group(g, g)

            def shift_rows(i, c):
                n = 6 * i + c
                sp.wait_ge(m_split, n + 1)
                sp.dma_start(shift_dram[c % 2].rearrange("k a t -> a k t"), m_parts[:, c % 2]).then_inc(m_stored, 16)
                sp.wait_ge(m_stored, 16 * n + 16)
                sp.dma_start(q_sb[buf(c)][SHIFT:SHIFT + PARTS, c % 2].rearrange("r h q -> r (h q)"),
                               shift_dram[c % 2].rearrange("k a t -> k (a t)")).then_inc(m_in, 16)

            sp.wait_ge(qk_in[0], LOADS)
            shift_rows(0, 0)

            def step(i, c, n):
                if c % 2 == 0 and c >= 2 and (n is None or n + 4 < NH):
                    sp.wait_ge(scores_ready, 8 * KT * group(i, c))
                    load_group(group(i, c + 4), buf(c + 4))
                if n is None or n + 1 < NH:
                    shift_rows(i, c + 1)
            over_halves(sp, step)

            sp.wait_ge(attn_ready, NH)
            for s in range(2):
                sp.dma_start(late_tile(s, 3).rearrange("p (q e) -> p q e", e=E), x_c[s]).then_inc(x2_in[s], 16)
            with sp.Fori(0, NC // 2 - 1) as i:
                for s in range(2):
                    sp.wait_ge(y_ready[s], i + 1)
                    sp.dma_start(out_c[bass.ds(2 * i + s, 1)].rearrange("c p q e -> (c p) q e"),
                                 late_tile(2, s).rearrange("p (q e) -> p q e", e=E)).then_inc(y_out[s], 16)
                    sp.dma_start(late_tile(s, 3).rearrange("p (q e) -> p q e", e=E),
                                 x_c[bass.ds(2 * i + s + 2, 1)].rearrange("c p q e -> (c p) q e")).then_inc(x2_in[s], 16)
            for s in range(2):
                sp.wait_ge(y_ready[s], NC // 2)
                sp.dma_start(out_c[NC - 2 + s], late_tile(2, s).rearrange("p (q e) -> p q e", e=E)).then_inc(y_out[s], 16)
            for s in range(2):
                sp.wait_ge(y_out[s], 16 * (NC // 2))

        @block.gpsimd
        def _(pool):
            pool.memset(ident[:, :], 0.0).then_inc(ident_step, 1)
            pool.memset(zero[:, :], 0.0).then_inc(ident_step, 1)
            pool.wait_ge(ident_step, 2)
            pool.affine_select(out=ident[:, :], in_=ident[:, :], compare_op=ALU.not_equal, fill=1.0, base=0,
                               pattern=[[-1, P]], channel_multiplier=1).then_inc(ident_step, 1)
            pool.wait_ge(ident_step, 3)
            def copy(to, of, shape):
                zero_bc = zero[:, :] if len(shape) == 1 else zero[:, :].rearrange("p (a b) -> p a b", a=1) \
                    if len(shape) == 2 else zero[:, :].rearrange("p (a b c) -> p a b c", a=1, b=1)
                return pool.tensor_tensor(to, of, zero_bc.broadcast_to([P, *shape]), ALU.add)

            with pool.Fori(0, NC // 2) as i:
                for s in range(2):
                    pool.wait_ge(xnT_st_ready[s], i + 1)
                    copy(xnT_attn[:, bass.ds((2 * i + s) * CH, CH)], xnT_st[:, s, :], [CH]).then_inc(xnT_ready[s], 1)

            def fill_v(g, s):
                copy(vx[s][:, :, :, 0:D],
                                 v_all[:, :, :, :, :].rearrange("p b g k (h d) -> p (b g) k h d", d=D)[:, bass.ds(g, 1)]
                     .rearrange("p a k h d -> p (a k) h d"), [KT, HG, D]).then_inc(vx_ready, 1)
            for s in range(2):
                pool.wait_ge(xnT_ready[s], NC // 2)
            steps = 0
            for s in range(NBUF):
                for rows, z, value in ((slice(64, 96), 0, 0.0), (slice(64, 96), 1, 0.0),
                                       (slice(96, 128), 0, 0.0), (slice(96, 128), 1, 1.0)):
                    if steps:
                        pool.wait_ge(rows_const, steps)
                    pool.memset(qk_buf[rows, s, z], value).then_inc(rows_const, 1)
                    steps += 1
            pool.wait_ge(rows_const, steps)
            for s in range(NBUF):
                pool.memset(vx[s][:, :, :, D + 1:32], 0.0)
                pool.memset(vx[s][:, :, :, D:D + 1], 1.0).then_inc(vx_const, 1)
            for s in range(2):
                pool.wait_ge(v_ready[s], NC // 2)
            pool.wait_ge(vx_const, NBUF)
            for g in range(NBUF):
                fill_v(g, g)

            with pool.Fori(0, NC // 2) as i:
                for s in range(2):
                    for z in range(2):
                        m = 4 * (4 * i + 2 * s + z)
                        part = qk_p[:, s, z]
                        pool.wait_ge(qk_f_ready[z], 2 * i + s + 1)
                        pool.wait_ge(parts_stored[s], 16 * 2 * PARTS * i)
                        copy(part[:, 0], qk_f[:, z], [CH]).then_inc(split_step, 1)
                        pool.wait_ge(split_step, m + 1)
                        pool.tensor_tensor(qk_r[:, 0], qk_f[:, z], part[:, 0], ALU.subtract).then_inc(split_step, 1)
                        pool.wait_ge(split_step, m + 2)
                        copy(part[:, 1], qk_r[:, 0], [CH]).then_inc(split_step, 1)
                        pool.wait_ge(split_step, m + 3)
                        pool.tensor_tensor(qk_r[:, 1], qk_r[:, 0], part[:, 1], ALU.subtract).then_inc(split_step, 1)
                        pool.wait_ge(split_step, m + 4)
                        copy(part[:, 2], qk_r[:, 1], [CH]).then_inc(parts_ready[z], 1)

            def step(i, c, n):
                if c % 2 == 0 and c >= 2 and (n is None or n + 4 < NH):
                    pool.wait_ge(pv_done, 16 * group(i, c))
                    fill_v(group(i, c + 4), buf(c + 4))
            over_halves(pool, step)

        @block.scalar
        def _(act):
            act.wait_ge(var_ready, 1)
            act.activation(mom[:, 4, :], mom[:, 3, :], ACT.Sqrt).then_inc(std_ready, 1)
            act.wait_ge(rw_T, 1)
            act.activation(rwT[:, :], ps[:, 6, 0:NE], ACT.Copy).then_inc(rw_ready, 1)
            with act.Fori(0, NC // 2) as i:
                for s in range(2):
                    act.wait_ge(xn_T[s], i + 1)
                    act.wait_ge(v_ps[s], i)
                    act.wait_ge(xnT_ready[s], i)
                    act.activation(xnT_st[:, s, :], ps[:, s, :], ACT.Copy).then_inc(xnT_st_ready[s], 1)
            act.wait_ge(gexp_in, 1)
            act.activation(gm[:, 2], gm[:, 1], ACT.Exp).then_inc(gexp_out, 1)
            act.wait_ge(gate_Tps, 1)
            act.activation(gate_T[:, :, :], ps[:, 6, 0:2 * P].rearrange("p (k t) -> p k t", k=2), ACT.Copy).then_inc(gate_Tsb, 1)
            with act.Fori(0, NC // 2) as i:
                for s in range(2):
                    c = 2 * i + s
                    for j in range(16):
                        k = j % 2
                        act.wait_ge(gu_ready[k], 8 * c + j // 2 + 1)
                        act.wait_ge(hu_ready[k], 8 * c + j // 2)
                        act.activation(silu[:, k, :], ps[:, k, :], ACT.Silu).then_inc(silu_ready[k], 1)
                    for z in range(2):
                        act.wait_ge(qk_ps[z], c + 1)
                        act.wait_ge(parts_ready[z], c)
                        act.activation(qk_f[:, z, :], ps[:, 6 + z, :], ACT.Identity, bias=bqk[:, z:z + 1],
                                       scale=SCALE if z == 0 else 1.0).then_inc(qk_f_ready[z], 1)
                    act.wait_ge(down_done[3], 4 * c + 4)
                    act.activation(x_ffn[:, bass.ds(c * CH, CH)], ps[:, 4 + s, :], ACT.Copy).then_inc(ffn_ready[s], 1)

            def step(i, c, n):
                for kt in range(KT):
                    u = KT * (6 * i + c) + kt
                    for h in range(HG):
                        act.wait_ge(scores_ready, 4 * u + h + 1)
                        if h == 0 and (n is None or u >= 2):
                            act.wait_ge(pv_done, u - 1)
                        act.activation(probs[:, kt % 2, h], ps[:, h % 2, :], ACT.Exp).then_inc(exp_done, 1)
                    if kt == 0 and (n is None or n >= 1):
                        evacuate(i, c - 1, n is None or n >= 3)

            def evacuate(i, c, reused):
                n = 6 * i + c
                act.wait_ge(pv_done, 8 * n + 8)
                if reused:
                    act.wait_ge(o_T, n - 1)
                act.activation(oT[:, c % 2, :], ps[:, 6, :], ACT.Copy).then_inc(o_out, 1)

            over_halves(act, step)
            evacuate(0, NH - 1, True)

            with act.Fori(0, NC // 2) as i:
                for s in range(2):
                    act.wait_ge(a_T[s], i + 1)
                    act.wait_ge(a_proj[s], i)
                    act.activation(late_tile(s, 1), ps[:, s, :], ACT.Copy).then_inc(a_sb[s], 1)

        @block.vector
        def _(dve):
            step_no = [0]

            def then(ins):
                step_no[0] += 1
                ins.then_inc(mom_step, 1)
                dve.wait_ge(mom_step, step_no[0])

            dve.memset(rank[:, :], 0.0).then_inc(const_step, 1)
            dve.wait_ge(const_step, 1)
            for e in range(NE):
                dve.memset(rank[:, e:e + 1], float(NE - e)).then_inc(const_step, 1)
            for k in range(4):
                dve.wait_ge(x_in[k], 16)
                with dve.Fori(k * NT // 4, (k + 1) * NT // 4) as n:
                    dve.bn_stats(stats[:, bass.ds(n, 1), :].rearrange("p a s -> p (a s)"),
                                 x_all[:, bass.ds(n, 1), :].rearrange("p a e -> p (a e)")).then_inc(stat_done, 1)
            dve.wait_ge(stat_done, NT)
            mean_e, m2_e, mean_o, m2_o = (stats[:, :, k] for k in (1, 2, 4, 5))
            then(dve.tensor_tensor(mom[:, 0, :], mean_e, mean_o, ALU.add))
            then(dve.tensor_scalar(mom[:, 0, :], mom[:, 0, :], 0.5, None, ALU.mult))
            then(dve.tensor_tensor(mom[:, 1, :], mean_e, mean_o, ALU.subtract))
            then(dve.scalar_tensor_tensor(mom[:, 1, :], mom[:, 1, :], 0.25, mom[:, 1, :], ALU.mult, ALU.mult))
            then(dve.tensor_tensor(mom[:, 2, :], m2_e, m2_o, ALU.add))
            then(dve.scalar_tensor_tensor(mom[:, 2, :], mom[:, 2, :], 1.0 / E, mom[:, 1, :], ALU.mult, ALU.add))
            dve.tensor_scalar(mom[:, 3, :], mom[:, 2, :], EPS, None, ALU.add).then_inc(var_ready, 1)
            dve.wait_ge(std_ready, 1)
            then(dve.reciprocal(mom[:, 1, :], mom[:, 4, :]))

            dve.wait_ge(proj_in, 64)
            for z, w in enumerate((wq_in, wk_in)):
                dve.tensor_copy(wqk[:, z, :].rearrange("p (g d h) -> p g d h", g=HG, d=D),
                                w[:, :].rearrange("p (g h d) -> p g d h", g=HG, h=HG)).then_inc(const_step, 1)
            dve.wait_ge(small_in, 16 * (3 + 2 * HG * D))
            dve.tensor_scalar(bqk[:, 0:1], bq_in[:, :], SCALE, None, ALU.mult).then_inc(const_step, 1)

            with dve.Fori(0, NC // 2) as i:
                for s in range(2):
                    dve.wait_ge(xn_T[s], i)
                    for j in range(TPC):
                        n = (2 * i + s) * TPC + j
                        ins = dve.tensor_scalar(xn[:, s, j, :], x_all[:, bass.ds(n, 1), :].rearrange("p a e -> p (a e)"),
                                                mom[:, 0, bass.ds(n, 1)], mom[:, 1, bass.ds(n, 1)],
                                                ALU.subtract, ALU.mult)
                    ins.then_inc(xn_ready[s], 1)
                for s in range(2):
                    c = 2 * i + s
                    dve.wait_ge(v_ps[s], i + 1)
                    dve.tensor_copy(lg[:, bass.ds(c * TPC, TPC), :],
                                    ps[:, 4 + s, 0:TPC * NE].rearrange("p (j e) -> p j e", e=NE))
                    dve.tensor_tensor(v_all[:, bass.ds(i, 1), :, s * TPC:(s + 1) * TPC, :]
                                      .rearrange("p b g k c -> p (b k) g c"),
                                      ps[:, 2 + s, :].rearrange("p (k g c) -> p k g c", k=TPC, g=HG),
                                      bv_row[:, :].rearrange("p (a g c) -> p a g c", a=1, g=HG)
                                      .broadcast_to([P, TPC, HG, HG * D]), ALU.add).then_inc(v_ready[s], 1)

            for s in range(2):
                dve.wait_ge(v_ready[s], NC // 2)
            dve.wait_ge(const_step, NE + 1)
            rank_bc = rank[:, :].rearrange("p (a e) -> p a e", a=1).broadcast_to([P, NT, NE])

            def bc(v):
                return v.rearrange("p (n a) -> p n a", a=1).broadcast_to([P, NT, NE])

            def largest(logits, k):
                then(dve.tensor_reduce(gm[:, 0, k, :], logits, AX.X, ALU.max))
                then(dve.tensor_tensor(gt[:, 0], logits, bc(gm[:, 0, k, :]), ALU.is_equal))
                then(dve.tensor_tensor(gt[:, 0], gt[:, 0], rank_bc, ALU.mult))
                then(dve.tensor_reduce(gm[:, 7, k, :], gt[:, 0], AX.X, ALU.max))
                then(dve.tensor_tensor(gt[:, 1 + k], rank_bc, bc(gm[:, 7, k, :]), ALU.is_equal))

            largest(lg[:, :, :], 0)
            then(dve.tensor_scalar(gt[:, 3], gt[:, 1], -2.0 * BIG, BIG, ALU.mult, ALU.add))
            then(dve.tensor_tensor(gt[:, 3], gt[:, 3], lg[:, :, :], ALU.min))
            largest(gt[:, 3], 1)
            dve.tensor_scalar(gm[:, 1], gm[:, 0], -1.0, 80.0, ALU.mult, ALU.min).then_inc(gexp_in, 1)
            dve.wait_ge(gexp_out, 1)
            then(dve.tensor_scalar(gm[:, 3], gm[:, 2], 1.0, None, ALU.add))
            then(dve.reciprocal(gm[:, 4], gm[:, 3]))
            then(dve.tensor_tensor(gm[:, 5, 0, :], gm[:, 4, 0, :], gm[:, 4, 1, :], ALU.add))
            then(dve.tensor_scalar(gm[:, 5, 0, :], gm[:, 5, 0, :], 1e-10, None, ALU.add))
            then(dve.reciprocal(gm[:, 5, 1, :], gm[:, 5, 0, :]))
            for k in range(2):
                then(dve.tensor_tensor(gm[:, 6, k, :], gm[:, 4, k, :], gm[:, 5, 1, :], ALU.mult))
            for k in range(2):
                then(dve.tensor_tensor(gt[:, 4 + k], gt[:, 1 + k], bc(gm[:, 6, k, :]), ALU.mult))
            dve.tensor_tensor(gate_en[:, :, :].rearrange("p e n -> p n e"), gt[:, 4], gt[:, 5], ALU.add).then_inc(gate_ready, 1)

            with dve.Fori(0, NC // 2) as i:
                for s in range(2):
                    c = 2 * i + s
                    for j in range(16):
                        k, r, e = j % 2, j // 4, (j // 2) % 2
                        dve.wait_ge(silu_ready[k], 8 * c + j // 2 + 1)
                        dve.tensor_tensor(hu[:, k, :], silu[:, k, :], ps[:, 2 + k, :], ALU.mult).then_inc(hu_ready[k], 1)
                        if j % 4 == 0:
                            dve.wait_ge(gate_in[r], 16 * c + 16)
                        dve.wait_ge(hu_ready[k], 8 * c + j // 2 + 1)
                        dve.wait_ge(down_done[j % 4], 4 * c + j // 4)
                        dve.tensor_tensor(hid[:, j % 4, :], hu[:, k, :], gate_bc[:, r, e, :], ALU.mult).then_inc(hid_ready[j % 4], 1)

            def maxima(i, c, kt, reused=True):
                n = 6 * i + c
                if kt == 0 and reused:
                    dve.wait_ge(m_T, n - 1)
                for r in (2 * kt, 2 * kt + 1):
                    dve.wait_ge(x_ready, 16 * n + r + 1)
                    dve.tensor_reduce(mneg[:, c % 2, r:r + 1], ps[:, 2 + 2 * (r % 2):4 + 2 * (r % 2), :], AX.XY, ALU.max,
                                      negate=True).then_inc(max_done, 1)

            def split_max(i, c, reused):
                n, k = 6 * i + c, c % 2
                src = ps[0:HG * TPC, 7, 0:P]
                dve.wait_ge(m_T, n + 1)
                if reused:
                    dve.wait_ge(m_stored, 16 * n - 16)
                dve.tensor_copy(m_parts[:, k, 0], src).then_inc(m_hi, 1)
                dve.wait_ge(m_hi, n + 1)
                dve.tensor_tensor(m_rest[:, 0], src, m_parts[:, k, 0], ALU.subtract).then_inc(m_read, 1)
                dve.wait_ge(m_read, n + 1)
                dve.tensor_copy(m_parts[:, k, 1], m_rest[:, 0]).then_inc(m_mid, 1)
                dve.wait_ge(m_mid, n + 1)
                dve.tensor_tensor(m_rest[:, 1], m_rest[:, 0], m_parts[:, k, 1], ALU.subtract).then_inc(m_rest2, 1)
                dve.wait_ge(m_rest2, n + 1)
                dve.tensor_copy(m_parts[:, k, 2], m_rest[:, 1]).then_inc(m_split, 1)

            def divide(i, c):
                n = 6 * i + c
                o = ps[:, 7, :].rearrange("p (a c) -> p a c", c=32)
                dve.wait_ge(o_T, n + 1)
                dve.reciprocal(recip[:, c % 2, :], o[:, :, D:D + 1].rearrange("p a c -> p (a c)")).then_inc(recip_ready, 1)
                dve.wait_ge(recip_ready, n + 1)
                dve.tensor_tensor(attn_all[:, bass.ds(n, 1), :, :].rearrange("p n q (h d) -> p (n q h) d", d=D),
                                  o[:, :, 0:D],
                                  recip[:, c % 2, :].rearrange("p (a c) -> p a c", c=1).broadcast_to([P, HG * TPC, D]),
                                  ALU.mult).then_inc(attn_ready, 1)

            for c in range(2):
                for kt in range(KT):
                    maxima(0, c, kt, False)
            split_max(0, 0, False)

            def step(i, c, n):
                for kt in range(KT):
                    if n is None or n + 2 < NH:
                        maxima(i, c + 2, kt)
                    if kt == 3 and (n is None or n + 1 < NH):
                        split_max(i, c + 1, n is None or n >= 1)
                    if kt == 6 and (n is None or n >= 1):
                        divide(i, c - 1)
            over_halves(dve, step)
            divide(0, NH - 1)

            dve.wait_ge(attn_ready, NH)

            with dve.Fori(0, NC // 2) as i:
                for s in range(2):
                    dve.wait_ge(a_T[s], i)
                    for q in range(TPC):
                        ins = dve.tensor_copy(late_tile(s, 0)[:, q * E:(q + 1) * E].rearrange("p (g c) -> p g c", g=HG),
                                              xnT_attn[:, :].rearrange("p (b g a q c) -> p b a q g c", b=B, g=HG, a=2, q=TPC)
                                              [:, bass.ds(i, 1), s, q].rearrange("p b g c -> p (b g) c"))
                    ins.then_inc(a_staged[s], 1)
                for s in range(2):
                    dve.wait_ge(a_proj[s], i + 1)
                    dve.wait_ge(y_T[s], i)
                    dve.scalar_tensor_tensor(late_tile(s, 2), ps[:, 2 + s, :], bo_col[:, 0:1],
                                             x_ffn[:, bass.ds((2 * i + s) * CH, CH)], ALU.add, ALU.add).then_inc(y_T_in[s], 1)
                for s in range(2):
                    dve.wait_ge(y_T[s], i + 1)
                    dve.wait_ge(x2_in[s], 16 * i + 16)
                    dve.wait_ge(y_out[s], 16 * i)
                    dve.tensor_tensor(late_tile(2, s), ps[:, 4 + s, :], late_tile(s, 3), ALU.add).then_inc(y_ready[s], 1)

        @block.tensor
        def _(pe):
            pe.wait_ge(ident_step, 3)
            pe.wait_ge(small_in, 16 * (3 + 2 * HG * D))
            pe.transpose(ps[:, 6, 0:NE], rw_in[:, :], ident[0:NE, 0:NE]).then_inc(rw_T, 1)
            pe.wait_ge(rw_ready, 1)
            pe.wait_ge(proj_in, 64)

            with pe.Fori(0, NC // 2) as i:
                for s in range(2):
                    pe.wait_ge(xn_ready[s], i + 1)
                    pe.wait_ge(xnT_st_ready[s], i)
                    for j in range(TPC):
                        mm = pe.transpose(ps[:, s, j * P:(j + 1) * P], xn[:, s, j, :], ident[:, :])
                    mm.then_inc(xn_T[s], 1)
                for s in range(2):
                    pe.wait_ge(xnT_st_ready[s], i + 1)
                    pe.wait_ge(v_ready[s], i)
                    for j in range(TPC):
                        tok = xnT_st[:, s, j * P:(j + 1) * P]
                        pe.matmul(ps[:, 4 + s, j * NE:(j + 1) * NE], tok, rwT[:, :], start=True, stop=True)
                        mm = pe.matmul(ps[:, 2 + s, j * E:(j + 1) * E], tok, wv[:, :], start=True, stop=True)
                    mm.then_inc(v_ps[s], 1)
            pe.wait_ge(gate_ready, 1)
            for k in range(2):
                mm = pe.transpose(ps[:, 6, k * P:(k + 1) * P],
                                  gate_en[:, 4 * k:4 * k + 4, :].rearrange("p e n -> p (e n)"), ident[:, :])
            mm.then_inc(gate_Tps, 1)
            pe.wait_ge(gate_Tsb, 1)

            pe.wait_ge(ffn_in, 48)
            pe.wait_ge(const_step, NE + 4)
            for s in range(2):
                pe.wait_ge(xnT_ready[s], NC // 2)
            with pe.Fori(0, NC // 2) as i:
                for s in range(2):
                    c = 2 * i + s
                    tokens = xnT_attn[:, bass.ds(c * CH, CH)]

                    def down(j):
                        pe.wait_ge(hid_ready[j % 4], 4 * c + j // 4 + 1)
                        if j == 0:
                            pe.wait_ge(ffn_ready[s], i)
                        pe.matmul(ps[:, 4 + s, :], w_dn[:, j // 2, j % 2, :], hid[:, j % 4, :],
                                  start=(j == 0), stop=(j == 15)).then_inc(down_done[j % 4], 1)

                    def project(z):
                        pe.wait_ge(qk_f_ready[z], c)
                        pe.matmul(ps[:, 6 + z, :], wqk[:, z, :], tokens, start=True, stop=True).then_inc(qk_ps[z], 1)

                    for j in range(16):
                        k, e, f = j % 2, j // 2, (j % 2) * P
                        pe.wait_ge(hu_ready[k], 8 * c + j // 2)
                        pe.matmul(ps[:, k, :], w_gu[:, 0, e, f:f + P], tokens, start=True, stop=True)
                        pe.matmul(ps[:, 2 + k, :], w_gu[:, 1, e, f:f + P], tokens, start=True, stop=True).then_inc(gu_ready[k], 1)
                        if j >= 2:
                            down(j - 2)
                    project(0)
                    down(14)
                    project(1)
                    down(15)

            for s in range(2):
                pe.wait_ge(ffn_ready[s], NC // 2)
                pe.wait_ge(qk_f_ready[s], NC)
            pe.wait_ge(rows_const, 4 * NBUF)

            def maxima(i, c, r):
                n, s = 6 * i + c, buf(c)
                if r == 0 and c % 2 == 0:
                    pe.wait_ge(qk_in[s], LOADS * (turn(i, c) + 1))
                h, q = r // TPC, r % TPC
                if c >= 1 or r >= 2:
                    pe.wait_ge(max_done, 16 * n + r - 1)
                for half in range(2):
                    mm = pe.matmul(ps[:, 2 + 2 * (r % 2) + half, :], q_sb[s][0:KX, c % 2, h, q * P:(q + 1) * P],
                                   k_sb[s][0:KX, half, h, :], start=True, stop=True)
                mm.then_inc(x_ready, 1)

            def turn_max(i, c, first):
                n = 6 * i + c
                pe.wait_ge(max_done, 16 * n + 16)
                if not first:
                    pe.wait_ge(attn_ready, n - 2)
                pe.transpose(ps[0:HG * TPC, 7, 0:P], mneg[:, c % 2, :], ident[:, :]).then_inc(m_T, 1)

            def turn_output(i, c):
                n = 6 * i + c
                pe.wait_ge(o_out, n + 1)
                if type(n) is int and n >= NH - 2:
                    pe.wait_ge(attn_ready, n)
                else:
                    pe.wait_ge(m_read, n + 3)
                for q in range(TPC):
                    mm = pe.transpose(ps[:, 7, q * P:(q + 1) * P], oT[:, c % 2, q * P:(q + 1) * P], ident[:, :])
                mm.then_inc(o_T, 1)

            def scores(i, c, kt, h, first):
                n, s = 6 * i + c, buf(c)
                if kt == 0 and h == 0:
                    pe.wait_ge(m_in, 16 * n + 16)
                if not first:
                    pe.wait_ge(exp_done, 4 * (KT * n + kt) + h - 1)
                pe.matmul(ps[:, h % 2, :], k_sb[s][0:KS, kt // 4, h, kt % 4 * P:(kt % 4 + 1) * P],
                          q_sb[s][0:KS, c % 2, h, :], start=True, stop=True).then_inc(scores_ready, 1)

            def weigh(i, c, kt):
                n, s = 6 * i + c, buf(c)
                pe.wait_ge(exp_done, 4 * (KT * n + kt) + 4)
                if kt == 0:
                    if c >= 1:
                        pe.wait_ge(o_out, n)
                    if c % 2 == 0:
                        pe.wait_ge(vx_ready, group(i, c) + 1)
                for h in range(HG):
                    mm = pe.matmul(ps[32 * h:32 * h + 32, 6, :], vx[s][:, kt, h, :], probs[:, kt % 2, h, :],
                                   start=(kt == 0), stop=(kt == KT - 1))
                mm.then_inc(pv_done, 1)

            for c in range(2):
                for kt in range(KT):
                    for r in (2 * kt, 2 * kt + 1):
                        maxima(0, c, r)
            turn_max(0, 0, True)

            def step(i, c, n):
                for kt in range(KT):
                    for h in range(2):
                        scores(i, c, kt, h, n == 0 and kt == 0)
                    if n is None or n + 2 < NH:
                        maxima(i, c + 2, 2 * kt)
                    if kt >= 1:
                        weigh(i, c, kt - 1)
                    elif n is None or n >= 1:
                        weigh(i, c - 1, KT - 1)
                    for h in range(2, HG):
                        scores(i, c, kt, h, False)
                    if n is None or n + 2 < NH:
                        maxima(i, c + 2, 2 * kt + 1)
                    if kt == 2 and (n is None or n + 1 < NH):
                        turn_max(i, c + 1, n is not None and n < 2)
                    if kt == 5 and (n is None or n >= 1):
                        turn_output(i, c - 1)
            over_halves(pe, step)
            weigh(0, NH - 1, KT - 1)
            turn_output(0, NH - 1)

            with pe.Fori(0, NC // 2) as i:
                for s in range(2):
                    pe.wait_ge(a_staged[s], i + 1)
                    pe.wait_ge(a_sb[s], i)
                    for q in range(TPC):
                        mm = pe.transpose(ps[:, s, q * P:(q + 1) * P], late_tile(s, 0)[:, q * P:(q + 1) * P], ident[:, :])
                    mm.then_inc(a_T[s], 1)
                for s in range(2):
                    pe.wait_ge(a_sb[s], i + 1)
                    pe.wait_ge(y_T_in[s], i)
                    pe.matmul(ps[:, 2 + s, :], wo[:, :], late_tile(s, 1), start=True, stop=True).then_inc(a_proj[s], 1)
                for s in range(2):
                    pe.wait_ge(y_T_in[s], i + 1)
                    pe.wait_ge(y_ready[s], i)
                    for q in range(TPC):
                        mm = pe.transpose(ps[:, 4 + s, q * P:(q + 1) * P], late_tile(s, 2)[:, q * P:(q + 1) * P], ident[:, :])
                    mm.then_inc(y_T[s], 1)


_INS = ["L0_attn_inputs", "L0_attn_Wq", "L0_attn_bq", "L0_attn_Wk", "L0_attn_bk", "L0_attn_Wv", "L0_attn_bv",
        "L0_attn_Wo", "L0_attn_bo", "L0_ffn_router_w", "L0_ffn_w_gate", "L0_ffn_w_up", "L0_ffn_w_down"]


def kernel(**inputs):
    import concourse.bacc as bacc
    from concourse.bass_utils import run_bass_kernel_spmd

    nc = bacc.Bacc("TRN2", target_bir_lowering=False, num_devices=1)
    arrays, args = {}, []
    for name in _INS:
        a = np.ascontiguousarray(inputs[name])
        arrays[name] = a
        args.append(nc.dram_tensor(name, a.shape, mybir.dt.from_np(a.dtype), kind="ExternalInput").ap())
    y = nc.dram_tensor("y", (B, S, E), F32, kind="ExternalOutput").ap()
    build(nc, *args, y)
    return run_bass_kernel_spmd(nc, [arrays], core_ids=[0]).results[0]["y"]
```

```python
from contextlib import ExitStack

import numpy as np
import concourse.bass as bass
from concourse import mybir

F32 = mybir.dt.float32
BF16 = mybir.dt.bfloat16
ALU = mybir.AluOpType
ACT = mybir.ActivationFunctionType
AX = mybir.AxisListType

P = 128
B, S, E = 4, 1024, 128
H = 16
D = E // H
NE = 8
F = 256
T = B * S
NT = T // P
CH = 512
NC = T // CH
TPC = CH // P
HG = 4
NG = B * H // HG
NH = 2 * NG
KT = S // P
PARTS = 3
ROWS = PARTS * PARTS * D
SHIFT = 96
KX = SHIFT
KS = SHIFT + PARTS
NBUF = 3
SCALE = float(np.float32(1.0) / np.sqrt(np.float32(D)))
EPS = 1e-5
BIG = 1.7e38
TWO_ONES = float(np.array([0x3F803F80], np.uint32).view(np.float32)[0])
TILES = 2 * NT + NE
BREAK = NH - 6
LOADS = 16 * (PARTS + PARTS * PARTS)


def build(nc, x, Wq, bq, Wk, bk, Wv, bv, Wo, bo, router_w, w_gate, w_up, w_down, out):
    ctx = ExitStack()
    with ctx:
        ctx.enter_context(nc.allow_non_contiguous_dma(reason="bias columns"))

        def sb(name, shape, dt=F32):
            return ctx.enter_context(nc.sbuf_tensor(name, shape, dt))

        def sem(name):
            return ctx.enter_context(nc.semaphore(name))

        def dram(name, shape, dt):
            return nc.dram_tensor(name, shape, dt).ap()

        parts_dram = [dram(f"{z}_parts", [B, HG, 2, PARTS, D * HG, CH], BF16) for z in "qk"]
        slots_dram = dram("slots", [TILES * P, E], F32)
        results_dram = dram("results", [TILES * P, E], F32)
        shift_dram = dram("shift", [2, PARTS, HG * TPC, P], BF16)

        x_sb = sb("x_sb", [P, T])
        x_all = x_sb[:, :].rearrange("p (n e) -> p n e", e=E)
        qk_f = sb("qk_f", [P, 2, T])
        attn_all = qk_f[:, 0, :].rearrange("p (n q c) -> p n q c", n=NH, q=TPC)
        picked = [x_all, qk_f[:, 1, :].rearrange("p (n e) -> p n e", e=E)]
        v_all = sb("v_all", [P, B, HG, KT, HG * D])
        w_gu = sb("w_gu", [P, NE, 2, F])
        xnT_all = w_gu[:, :, :, :].rearrange("p e a f -> p (e a f)")
        w_dn = sb("w_dn", [P, NE, F // P, E])
        probs = sb("probs", [P, 2, HG, CH])
        early = probs[:, :, :, :].rearrange("p u h q -> p (u h q)")
        gt = early[:, 0:6 * NT * NE].rearrange("p (k n e) -> p k n e", k=6, e=NE)
        slot_map = early[:, 6 * NT * NE:10 * NT * NE].rearrange("p (k e n) -> p k e n", k=4, e=NE)
        wq_in, wk_in, wo = (sb(n, [P, E]) for n in ("wq_in", "wk_in", "wo"))
        wvr = sb("wvr", [P, E + NE])
        wqk = sb("wqk", [P, 2, E])
        bqk = sb("bqk", [P, 2])
        b_in = sb("b_in", [2, 2, E])
        bo_row = sb("bo_row", [P, E])
        bv_all = sb("bv_all", [P, B, E])
        rw_in = sb("rw_in", [NE, E])
        ident = sb("ident", [P, P])
        rank = sb("rank", [P, NE])
        before = sb("before", [P, P], BF16)
        ones = sb("ones", [P, P], BF16)
        ones_f = sb("ones_f", [P, NE * NT])
        steps_i = sb("steps_i", [P, TILES], mybir.dt.int32)
        steps = sb("steps", [P, TILES])
        stats = sb("stats", [P, NT, 6])
        mom = sb("mom", [P, 5, NT])
        lg = sb("lg", [P, NT, NE])
        gm = sb("gm", [P, 8, 2, NT])
        chosen = sb("chosen", [P, NE, NT], BF16)
        counts = sb("counts", [P, 6, NE])
        over = early[:, 10 * NT * NE:11 * NT * NE].rearrange("p (e n) -> p e n", e=NE)
        tile_e = early[:, 11 * NT * NE:(11 * NT + TILES) * NE].rearrange("p (t e) -> p t e", e=NE)
        tile_f = sb("tile_f", [P, TILES])
        tile_expert = sb("tile_expert", [P, TILES], mybir.dt.int32)
        slot_f = sb("slot_f", [P, 2, NT])
        slot = sb("slot", [P, 2, NT], mybir.dt.uint32)
        shared = sb("shared", [P, 2560])
        xn = shared[:, 0:1024].rearrange("p (s j e) -> p s j e", s=2, e=E)
        xnT_st = shared[:, 1024:2048].rearrange("p (s t) -> p s t", s=2)
        zeros = shared[:, 0:1024]
        xg = shared[:, 0:512].rearrange("p (s e) -> p s e", s=4)
        xgT = shared[:, 512:768].rearrange("p (s e) -> p s e", s=2)
        silu = shared[:, 768:1280].rearrange("p (s f) -> p s f", s=2)
        hid = shared[:, 1280:1792].rearrange("p (s f) -> p s f", s=2)
        hidT = shared[:, 1792:2304].rearrange("p (s f) -> p s f", s=2)
        result = shared[:, 2304:2560].rearrange("p (s e) -> p s e", s=2)
        rest = sb("rest", [P, 2, CH])
        part = sb("part", [P, 2, PARTS, CH], BF16)
        qk_buf = sb("qk_buf", [P, NBUF, 2, 2, HG, CH], BF16)
        q_sb = [qk_buf[:, s, 0] for s in range(NBUF)]
        k_sb = [qk_buf[:, s, 1] for s in range(NBUF)]
        vx = [sb(f"vx{s}", [P, KT, HG, 32]) for s in range(NBUF)]
        mneg = sb("mneg", [P, 2, HG * TPC])
        m_parts = sb("m_parts", [HG * TPC, 2, PARTS, P], BF16)
        m_rest = sb("m_rest", [HG * TPC, 2, P])
        oT = sb("oT", [P, 2, CH])
        recip = sb("recip", [P, 2, HG * TPC])
        late = [qk_buf[:, s].rearrange("p z a h q -> p (z a h q)").bitcast(F32) for s in range(NBUF)]

        def late_tile(s, k):
            return late[s][:, k * CH:(k + 1) * CH]

        ps = ctx.enter_context(nc.psum_tensor("ps", [P, 8, CH], F32))
        v_lg = ps[:, 2:6, 0:2 * (E + NE)].rearrange("p (s b) (j e) -> p s b j e", s=2, j=2)

        x_t = x.rearrange("b (m p) e -> p (b m) e", p=P)
        out_c = out.rearrange("b (a q p) e -> (b a) p q e", a=2, q=TPC)
        x_c = x.rearrange("b (a q p) e -> (b a) p q e", a=2, q=TPC)

        def sems(name, n=2):
            return [sem(f"{name}{k}") for k in range(n)]

        x_in, proj_in, small_in, ffn_in = sems("x_in", 4), sem("proj_in"), sem("small_in"), sem("ffn_in")
        ident_step, const_step, stat_done, mom_step = (sem(n) for n in ("ident_step", "const_step", "stat_done", "mom_step"))
        var_ready, std_ready, rw_T, rw_ready = (sem(n) for n in ("var_ready", "std_ready", "rw_T", "rw_ready"))
        xn_kept, xnT_kept, lg_ready = (sems(n) for n in ("xn_kept", "xnT_kept", "lg_ready"))
        bias_T = sem("bias_T")
        xn_ready, xn_T, xnT_ready, v_ps, v_ready = (sems(n) for n in ("xn_ready", "xn_T", "xnT_ready", "v_ps", "v_ready"))
        qk_ps, qk_ready, split_step, part_ready = sems("qk_ps"), sems("qk_ready"), sems("split_step"), sems("part_ready")
        split_late, first_stored, late_stored, qk_in = sems("split_late"), sems("first_stored"), sems("late_stored"), sems("qk_in", NBUF)
        gexp_in, gexp_out, chosen_ready, ranks_ps = (sem(n) for n in ("gexp_in", "gexp_out", "chosen_ready", "ranks_ps"))
        zeros_ready, zeros_stored, steps_ready, before_step = (sem(n) for n in (
            "zeros_ready", "zeros_stored", "steps_ready", "before_step"))
        routed, scattered, picked_in, mixed_step = (sem(n) for n in ("routed", "scattered", "picked_in", "mixed_step"))
        rows_const, vx_const, vx_ready = sem("rows_const"), sem("vx_const"), sem("vx_ready")
        scores_ready, exp_done, pv_done = sem("scores_ready"), sem("exp_done"), sem("pv_done")
        x_ready, max_done, m_T = (sem(n) for n in ("x_ready", "max_done", "m_T"))
        m_hi, m_read, m_mid, m_rest2, m_split = (sem(n) for n in ("m_hi", "m_read", "m_mid", "m_rest2", "m_split"))
        m_stored, m_in = sem("m_stored"), sem("m_in")
        o_out, o_T, recip_ready, attn_ready = (sem(n) for n in ("o_out", "o_T", "recip_ready", "attn_ready"))
        xg_in, xg_T = sems("xg_in", 4), sems("xg_T", 4)
        xgT_ready, gu_ready, silu_ready, hid_ready, hid_T, hidT_ready, down_done, result_ready, result_out = (
            sems(n) for n in ("xgT_ready", "gu_ready", "silu_ready", "hid_ready", "hid_T", "hidT_ready", "down_done",
                              "result_ready", "result_out"))
        a_staged, a_T, a_sb, a_proj, a_sum, y_ready = (sems(n) for n in (
            "a_staged", "a_T", "a_sb", "a_proj", "a_sum", "y_ready"))
        x2_in, x2_ready, y_out = sems("x2_in"), sems("x2_ready"), sems("y_out")

        def past(eng, s, k, unit=1):
            if type(k) is not int or k > 0:
                eng.wait_ge(s, unit * k)

        def over_pairs(eng, pair):
            pair(0)
            with eng.Fori(1, NC // 2 - 1) as i:
                pair(i)
            pair(NC // 2 - 1)

        def over_tiles(eng, tile):
            for k in range(4):
                tile(0, k)
            with eng.Fori(1, TILES // 4 - 1) as i:
                for k in range(4):
                    tile(i, k)
            for k in range(4):
                tile(TILES // 4 - 1, k)

        def exists(i, k):
            return type(i) is not int or 0 <= 4 * i + k < TILES

        def used(i, k, slots=2):
            return 4 // slots * i + k // slots

        def group(i, c):
            return 3 * i + c // 2

        def buf(c):
            return (c // 2) % NBUF

        def turn(i, c):
            return i + c // 2 // NBUF

        def over_halves(eng, step, experts=None):
            for c in range(2):
                step(0, c, c)
            with eng.Fori(0, (BREAK - 2) // 6) as i:
                for c in range(2, 8):
                    step(i, c, None)
            if experts:
                experts()
            for c in range(BREAK, NH):
                step(0, c, c)

        block = ctx.enter_context(nc.Block())

        @block.sync
        def _(sp):
            for k in range(4):
                n = NT // 4
                sp.dma_start(x_all[:, k * n:(k + 1) * n, :], x_t[:, k * n:(k + 1) * n, :]).then_inc(x_in[k], 16)
            sp.dma_start(rw_in[:, :], router_w).then_inc(small_in, 16)
            sp.dma_start(b_in[0:1, 0, :], bq.rearrange("(a e) -> a e", a=1)).then_inc(small_in, 16)
            sp.dma_start(b_in[1:2, 0, :], bk.rearrange("(a e) -> a e", a=1)).then_inc(small_in, 16)
            sp.dma_start(wvr[:, 0:E], Wv).then_inc(proj_in, 16)
            sp.dma_start(wq_in[:, :], Wq).then_inc(proj_in, 16)
            sp.dma_start(wk_in[:, :], Wk).then_inc(proj_in, 16)
            sp.dma_start(wo[:, :], Wo).then_inc(proj_in, 16)
            sp.dma_start(bv_all[:, :, :], bv.rearrange("(a b e) -> a b e", a=1, b=1).broadcast_to([P, B, E])).then_inc(small_in, 16)
            sp.dma_start(bo_row[:, :], bo.rearrange("(a e) -> a e", a=1).broadcast_to([P, E])).then_inc(small_in, 16)

            for c in range(2):
                for z in range(2):
                    sp.wait_ge(part_ready[z], c + 1)
                    for k in range(PARTS):
                        sp.dma_start(parts_dram[z][0, :, c, k], part[:, z, k]).then_inc(first_stored[z], 16)
            for z in range(2):
                sp.wait_ge(first_stored[z], 16 * 2 * PARTS)

            def load_group(g, s):
                k_src = parts_dram[1].rearrange("b g a k (d h) t -> (b g) (k d) a (h t)", h=HG)[bass.ds(g, 1)] \
                    .rearrange("g r a t -> (g r) a t")
                for copy in range(PARTS):
                    r = copy * PARTS * D
                    sp.dma_start(k_sb[s][r:r + PARTS * D].rearrange("r a h t -> r a (h t)"), k_src).then_inc(qk_in[s], 16)
                for part in range(PARTS):
                    q_src = parts_dram[0].rearrange("b g a k (d h) t -> (b g) k d a (h t)", h=HG)[bass.ds(g, 1), part] \
                        .rearrange("g r a t -> (g r) a t")
                    for copy in range(PARTS):
                        r = (part * PARTS + copy) * D
                        sp.dma_start(q_sb[s][r:r + D].rearrange("r a h t -> r a (h t)"), q_src).then_inc(qk_in[s], 16)

            sp.wait_ge(rows_const, 2 * NBUF)
            for g in range(NBUF):
                load_group(g, g)

            def shift_rows(i, c):
                n = 6 * i + c
                sp.wait_ge(m_split, n + 1)
                sp.dma_start(shift_dram[c % 2].rearrange("k a t -> a k t"), m_parts[:, c % 2]).then_inc(m_stored, 16)
                sp.wait_ge(m_stored, 16 * n + 16)
                sp.dma_start(q_sb[buf(c)][SHIFT:SHIFT + PARTS, c % 2].rearrange("r h q -> r (h q)"),
                               shift_dram[c % 2].rearrange("k a t -> k (a t)")).then_inc(m_in, 16)

            sp.wait_ge(qk_in[0], LOADS)
            shift_rows(0, 0)
            for z in range(2):
                sp.wait_ge(qk_ready[z], NC)
            for e in range(NE):
                sp.dma_start(w_gu[:, e, 0, :], w_gate[e]).then_inc(ffn_in, 16)
                sp.dma_start(w_gu[:, e, 1, :], w_up[e]).then_inc(ffn_in, 16)
            sp.dma_start(w_dn[:, :, :, :].rearrange("p e k d -> p (e k) d"),
                         w_down.rearrange("e (k p) d -> p (e k) d", p=P)).then_inc(ffn_in, 16)

            def step(i, c, n):
                if c % 2 == 0 and c >= 2 and (n is None or n + 4 < NH):
                    if c >= 4:
                        for z in range(2):
                            sp.wait_ge(late_stored[z], 16 * PARTS * (NC - 2))
                    sp.wait_ge(scores_ready, 8 * KT * group(i, c))
                    load_group(group(i, c + 4), buf(c + 4))
                if n is None or n + 1 < NH:
                    shift_rows(i, c + 1)

            def experts():
                def load(i, k):
                    sp.dma_start(xg[:, k % 4, :], slots_dram[bass.ds((4 * i + k) * P, P), :]).then_inc(xg_in[k % 4], 16)

                def tile(i, k):
                    if exists(i, k + 4):
                        sp.wait_ge(xg_T[k], used(i, k, 4) + 1)
                        load(i, k + 4)
                    if exists(i, k - 4):
                        store(i, k - 4)

                def store(i, k):
                    sp.wait_ge(result_ready[k % 2], used(i, k) + 1)
                    sp.dma_start(results_dram[bass.ds((4 * i + k) * P, P), :], result[:, k % 2, :]).then_inc(result_out[k % 2], 16)
                sp.wait_ge(scattered, 16 * 2 * NT)
                for k in range(4):
                    load(0, k)
                over_tiles(sp, tile)
                for k in range(4):
                    store(TILES // 4 - 1, k)
            over_halves(sp, step, experts)

            sp.wait_ge(attn_ready, NH)

            def load_x(c, s):
                sp.dma_start(late_tile(s, 3).rearrange("p (q e) -> p q e", e=E),
                             x_c[bass.ds(c, 1)].rearrange("c p q e -> (c p) q e")).then_inc(x2_in[s], 16)

            def store_y(c, s):
                sp.dma_start(out_c[bass.ds(c, 1)].rearrange("c p q e -> (c p) q e"),
                             late_tile(2, s).rearrange("p (q e) -> p q e", e=E)).then_inc(y_out[s], 16)
            for s in range(2):
                load_x(s, s)
            with sp.Fori(0, NC // 2 - 1) as i:
                for s in range(2):
                    sp.wait_ge(y_ready[s], i + 1)
                    store_y(2 * i + s, s)
                    load_x(2 * i + s + 2, s)
            for s in range(2):
                sp.wait_ge(y_ready[s], NC // 2)
                store_y(NC - 2 + s, s)
            for s in range(2):
                sp.wait_ge(y_out[s], 16 * (NC // 2))

        @block.gpsimd
        def _(pool):
            pool.memset(ident[:, :], 0.0).then_inc(ident_step, 1)
            pool.wait_ge(ident_step, 1)
            pool.affine_select(out=ident[:, :], in_=ident[:, :], compare_op=ALU.not_equal, fill=1.0, base=0,
                               pattern=[[-1, P]], channel_multiplier=1).then_inc(ident_step, 1)
            pool.wait_ge(ident_step, 2)
            k = 0
            words = [qk_buf[:, s].rearrange("p z a h q -> p z (a h q)").bitcast(F32) for s in range(NBUF)]
            for s in range(NBUF):
                for tile, value in ((words[s][64:SHIFT, :, :], 0.0), (words[s][SHIFT:P, 1, :], TWO_ONES)):
                    if k:
                        pool.wait_ge(rows_const, k)
                    pool.memset(tile, value).then_inc(rows_const, 1)
                    k += 1
            pool.wait_ge(rows_const, k)
            pool.iota(steps_i[:, :], [[1, TILES]], base=0, channel_multiplier=0).then_inc(steps_ready, 1)
            pool.memset(before[:, :], 1.0).then_inc(before_step, 1)
            pool.wait_ge(before_step, 1)
            pool.affine_select(out=before[:, :], in_=before[:, :], compare_op=ALU.is_ge, fill=0.0, base=-1,
                               pattern=[[1, P]], channel_multiplier=-1).then_inc(before_step, 1)

            def split(c, z, m, stored):
                pool.wait_ge(qk_ready[z], c + 1)
                if stored:
                    pool.wait_ge(*stored)
                f, r = qk_f[:, z, c * CH:(c + 1) * CH], rest[:, 1, :]
                for k in range(PARTS):
                    src = f if k == 0 else r
                    if k:
                        pool.wait_ge(split_step[1], 4 * m + 2 * k)
                    ins = pool.tensor_copy(part[:, z, k], src)
                    if k == PARTS - 1:
                        ins.then_inc(part_ready[z] if c < 2 else split_late[z], 1)
                    else:
                        ins.then_inc(split_step[1], 1)
                        pool.wait_ge(split_step[1], 4 * m + 2 * k + 1)
                        pool.tensor_tensor(r, src, part[:, z, k], ALU.subtract).then_inc(split_step[1], 1)

            for c in range(2):
                split(c, 1, c, (first_stored[1], 16 * PARTS) if c else None)
            m = 2
            for c in range(2, NC):
                for z in range(2):
                    done = 16 * PARTS * (c - 2)
                    split(c, z, m, (late_stored[z], done) if c > 2 else (first_stored[z], 16 * 2 * PARTS))
                    m += 1
                    pool.wait_ge(split_late[z], c - 1)
                    for k in range(PARTS):
                        pool.dma_start(parts_dram[z][c // 2, :, c % 2, k], part[:, z, k]).then_inc(late_stored[z], 16)

            for s in range(2):
                pool.wait_ge(v_ps[s], NC // 2)
            pool.memset(zeros, 0.0).then_inc(zeros_ready, 1)
            pool.wait_ge(zeros_ready, 1)
            pool.dma_start(slots_dram.rearrange("(p a c) e -> p a (c e)", p=P, c=8),
                           zeros.rearrange("p (a n) -> p a n", a=1).broadcast_to([P, TILES // 8, 8 * E])).then_inc(zeros_stored, 16)
            pool.wait_ge(zeros_stored, 16)
            pool.wait_ge(routed, 1)
            for k in range(2):
                for n in range(NT):
                    pool.indirect_dma_start(out=slots_dram, out_offset=bass.IndirectOffsetOnAxis(ap=slot[:, k, n:n + 1], axis=0),
                                            in_=x_all[:, n, :], in_offset=None).then_inc(scattered, 16)
            for s in range(2):
                pool.wait_ge(result_out[s], 16 * TILES // 2)
            pool.wait_ge(scattered, 16 * 2 * NT)
            for k in range(2):
                for n in range(NT):
                    pool.indirect_dma_start(out=picked[k][:, n, :], out_offset=None, in_=results_dram,
                                            in_offset=bass.IndirectOffsetOnAxis(ap=slot[:, k, n:n + 1], axis=0)).then_inc(picked_in, 16)
            pool.wait_ge(picked_in, 16 * 2 * NT)
            for k in range(2):
                pool.tensor_tensor(picked[k], picked[k], gm[:, 6, k, :].rearrange("p (n a) -> p n a", a=1)
                                   .broadcast_to([P, NT, E]), ALU.mult).then_inc(mixed_step, 1)
            pool.wait_ge(mixed_step, 2)
            pool.tensor_tensor(picked[0], picked[0], picked[1], ALU.add).then_inc(mixed_step, 1)
            pool.wait_ge(mixed_step, 3)
            pool.tensor_tensor(picked[0], picked[0], bo_row[:, :].rearrange("p (a e) -> p a e", a=1)
                               .broadcast_to([P, NT, E]), ALU.add).then_inc(mixed_step, 1)

        @block.scalar
        def _(act):
            act.wait_ge(var_ready, 1)
            act.activation(mom[:, 4, :], mom[:, 3, :], ACT.Sqrt).then_inc(std_ready, 1)
            act.wait_ge(rw_T, 1)
            act.activation(wvr[:, E:E + NE], ps[:, 6, 0:NE], ACT.Copy).then_inc(rw_ready, 1)

            def keep(i, s):
                act.wait_ge(xn_T[s], i + 1)
                act.activation(xnT_st[:, s, :], ps[:, s, :], ACT.Copy).then_inc(xnT_ready[s], 1)
                act.activation(xnT_all[:, bass.ds((2 * i + s) * CH, CH)], ps[:, s, :], ACT.Copy).then_inc(xnT_kept[s], 1)

            def bias(i, s):
                for z in range(2):
                    c = 2 * i + s
                    act.wait_ge(qk_ps[z], c + 1)
                    act.activation(qk_f[:, z, bass.ds(c * CH, CH)], ps[:, 6 + z, :], ACT.Identity, bias=bqk[:, z:z + 1],
                                   scale=SCALE if z == 0 else 1.0).then_inc(qk_ready[z], 1)

            def pair(i):
                for s in range(2):
                    if s == 0:
                        keep(i, 1)
                    elif type(i) is not int or i < NC // 2 - 1:
                        keep(i + 1, 0)
                    act.wait_ge(lg_ready[s], i + 1)
                    for b in range(2):
                        k = s * TPC + 2 * b
                        ins = act.activation(v_all[:, bass.ds(i, 1), :, k:k + 2, :].rearrange("p b g k c -> p (b k) g c"),
                                             v_lg[:, s, b, :, 0:E].rearrange("p k (g c) -> p k g c", g=HG), ACT.Copy)
                    ins.then_inc(v_ready[s], 1)
                    if type(i) is int and i == 0:
                        bias(0, s)
            act.wait_ge(const_step, NE + 5)
            keep(0, 0)
            over_pairs(act, pair)
            with act.Fori(1, NC // 2) as i:
                for s in range(2):
                    bias(i, s)
            act.wait_ge(gexp_in, 1)
            act.activation(gm[:, 2], gm[:, 1], ACT.Exp).then_inc(gexp_out, 1)
            act.wait_ge(routed, 1)

            def step(i, c, n):
                for kt in range(KT):
                    u = KT * (6 * i + c) + kt
                    for h in range(HG):
                        act.wait_ge(scores_ready, 4 * u + h + 1)
                        if h == 0 and (n is None or u >= 2):
                            act.wait_ge(pv_done, u - 1)
                        act.activation(probs[:, kt % 2, h], ps[:, h % 2, :], ACT.Exp).then_inc(exp_done, 1)
                    if kt == 0 and (n is None or n >= 1):
                        evacuate(i, c - 1)

            def evacuate(i, c):
                n = 6 * i + c
                act.wait_ge(pv_done, KT * n + KT)
                act.activation(oT[:, c % 2, :], ps[:, 6, :], ACT.Copy).then_inc(o_out, 1)


            def experts():
                def tile(i, k):
                    s = k % 2
                    act.wait_ge(gu_ready[s], used(i, k) + 1)
                    act.activation(silu[:, s, :], ps[:, s, 0:F], ACT.Silu).then_inc(silu_ready[s], 1)
                    if exists(i, k - 1):
                        turn_hidden(i, k - 1)

                def turn_hidden(i, k):
                    s = k % 2
                    act.wait_ge(hid_T[s], used(i, k) + 1)
                    act.activation(hidT[:, s, :], ps[:, 2 + s, 0:F], ACT.Copy).then_inc(hidT_ready[s], 1)
                over_tiles(act, tile)
                turn_hidden(TILES // 4 - 1, 3)
            over_halves(act, step, experts)
            evacuate(0, NH - 1)

            def pair(i):
                for s in range(2):
                    act.wait_ge(a_T[s], i + 1)
                    past(act, a_proj[s], i)
                    act.activation(late_tile(s, 1), ps[:, s, :], ACT.Copy).then_inc(a_sb[s], 1)
            over_pairs(act, pair)

        @block.vector
        def _(dve):
            step_no = [0]

            def then(ins):
                step_no[0] += 1
                ins.then_inc(mom_step, 1)
                dve.wait_ge(mom_step, step_no[0])

            dve.memset(ones[:, :], 1.0)
            dve.memset(ones_f[:, :], 1.0)
            dve.memset(rank[:, :], 0.0).then_inc(const_step, 1)
            dve.wait_ge(const_step, 1)
            for e in range(NE):
                dve.memset(rank[:, e:e + 1], float(NE - e)).then_inc(const_step, 1)
            for g in range(NBUF):
                dve.memset(vx[g][:, :, :, D:D + 1], 1.0)
                dve.memset(vx[g][:, :, :, D + 1:32], 0.0).then_inc(vx_const, 1)
            for k in range(4):
                dve.wait_ge(x_in[k], 16)
                for n in range(k * NT // 4, (k + 1) * NT // 4):
                    dve.bn_stats(stats[:, n, :], x_all[:, n, :]).then_inc(stat_done, 1)
            dve.wait_ge(stat_done, NT)
            mean_e, m2_e, mean_o, m2_o = (stats[:, :, k] for k in (1, 2, 4, 5))
            then(dve.tensor_tensor(mom[:, 0, :], mean_e, mean_o, ALU.add))
            then(dve.tensor_scalar(mom[:, 0, :], mom[:, 0, :], 0.5, None, ALU.mult))
            then(dve.tensor_tensor(mom[:, 1, :], mean_e, mean_o, ALU.subtract))
            then(dve.scalar_tensor_tensor(mom[:, 1, :], mom[:, 1, :], 0.25, mom[:, 1, :], ALU.mult, ALU.mult))
            then(dve.tensor_tensor(mom[:, 2, :], m2_e, m2_o, ALU.add))
            then(dve.scalar_tensor_tensor(mom[:, 2, :], mom[:, 2, :], 1.0 / E, mom[:, 1, :], ALU.mult, ALU.add))
            dve.tensor_scalar(mom[:, 3, :], mom[:, 2, :], EPS, None, ALU.add).then_inc(var_ready, 1)
            dve.wait_ge(std_ready, 1)
            then(dve.reciprocal(mom[:, 1, :], mom[:, 4, :]))

            dve.wait_ge(proj_in, 64)
            for z, w in enumerate((wq_in, wk_in)):
                dve.tensor_copy(wqk[:, z, :].rearrange("p (g d h) -> p g d h", g=HG, d=D),
                                w[:, :].rearrange("p (g h d) -> p g d h", g=HG, h=HG)).then_inc(const_step, 1)
            dve.wait_ge(small_in, 16 * 5)
            dve.tensor_copy(b_in[:, 1, :].rearrange("p (g d h) -> p g d h", g=HG, d=D),
                            b_in[:, 0, :].rearrange("p (g h d) -> p g d h", g=HG, h=HG)).then_inc(const_step, 1)
            dve.wait_ge(bias_T, 1)
            dve.tensor_scalar(bqk[:, 0:1], ps[:, 7, 0:1], SCALE, None, ALU.mult)
            dve.tensor_copy(bqk[:, 1:2], ps[:, 7, 1:2]).then_inc(const_step, 1)

            def norm(i, s):
                c = 2 * i + s
                for j in range(TPC):
                    n = c * TPC + j
                    ins = dve.tensor_scalar(xn[:, s, j, :], x_all[:, bass.ds(n, 1), :].rearrange("p a e -> p (a e)"),
                                            mom[:, 0, bass.ds(n, 1)], mom[:, 1, bass.ds(n, 1)],
                                            ALU.subtract, ALU.mult)
                ins.then_inc(xn_ready[s], 1)
                dve.wait_ge(xn_ready[s], i + 1)
                dve.tensor_scalar(x_all[:, bass.ds(c * TPC, TPC), :], xn[:, s], 1.0, None, ALU.mult).then_inc(xn_kept[s], 1)

            def split_q(c):
                dve.wait_ge(qk_ready[0], c + 1)
                if c:
                    dve.wait_ge(first_stored[0], 16 * PARTS)
                f, r = qk_f[:, 0, c * CH:(c + 1) * CH], rest[:, 0, :]
                for k in range(PARTS):
                    src = f if k == 0 else r
                    ins = dve.tensor_copy(part[:, 0, k], src)
                    if k == PARTS - 1:
                        ins.then_inc(part_ready[0], 1)
                    else:
                        ins.then_inc(split_step[0], 1)
                        dve.wait_ge(split_step[0], 4 * c + 2 * k + 1)
                        dve.tensor_tensor(r, src, part[:, 0, k], ALU.subtract).then_inc(split_step[0], 1)
                        dve.wait_ge(split_step[0], 4 * c + 2 * k + 2)

            def pair(i):
                for s in range(2):
                    if type(i) is not int or i < NC // 2 - 1:
                        dve.wait_ge(xn_T[s], i + 1)
                        norm(i + 1, s)
                    c = 2 * i + s
                    dve.wait_ge(v_ps[s], i + 1)
                    dve.tensor_scalar(lg[:, bass.ds(c * TPC, TPC), :].rearrange("p (b j) e -> p b j e", b=2),
                                      v_lg[:, s, :, :, E:E + NE], 1.0, None, ALU.mult).then_inc(lg_ready[s], 1)
                    if type(i) is int and i == 0:
                        split_q(c)
            for s in range(2):
                norm(0, s)
            over_pairs(dve, pair)

            def fill_v(g, s):
                dve.tensor_tensor(vx[s][:, :, :, 0:D],
                                  v_all[:, :, :, :, :].rearrange("p b g k (h d) -> p (b g) k h d", d=D)[:, bass.ds(g, 1)]
                                  .rearrange("p a k h d -> p (a k) h d"),
                                  bv_all[:, :, :].rearrange("p b (g h d) -> p (b g) h d", h=HG, d=D)[:, bass.ds(g, 1)]
                                  .broadcast_to([P, KT, HG, D]), ALU.add).then_inc(vx_ready, 1)

            for s in range(2):
                dve.wait_ge(lg_ready[s], NC // 2)
            dve.wait_ge(const_step, NE + 1)
            rank_bc = rank[:, :].rearrange("p (a e) -> p a e", a=1).broadcast_to([P, NT, NE])

            def bc(v):
                return v.rearrange("p (n a) -> p n a", a=1).broadcast_to([P, NT, NE])

            def largest(logits, k):
                then(dve.tensor_reduce(gm[:, 0, k, :], logits, AX.X, ALU.max))
                then(dve.tensor_tensor(gt[:, 0], logits, bc(gm[:, 0, k, :]), ALU.is_equal))
                then(dve.tensor_tensor(gt[:, 0], gt[:, 0], rank_bc, ALU.mult))
                then(dve.tensor_reduce(gm[:, 7, k, :], gt[:, 0], AX.X, ALU.max))
                then(dve.tensor_tensor(gt[:, 1 + k], rank_bc, bc(gm[:, 7, k, :]), ALU.is_equal))

            largest(lg[:, :, :], 0)
            then(dve.tensor_scalar(gt[:, 3], gt[:, 1], -2.0 * BIG, BIG, ALU.mult, ALU.add))
            then(dve.tensor_tensor(gt[:, 3], gt[:, 3], lg[:, :, :], ALU.min))
            largest(gt[:, 3], 1)
            dve.tensor_scalar(gm[:, 1], gm[:, 0], -1.0, 80.0, ALU.mult, ALU.min).then_inc(gexp_in, 1)
            dve.wait_ge(gexp_out, 1)
            then(dve.tensor_scalar(gm[:, 3], gm[:, 2], 1.0, None, ALU.add))
            then(dve.reciprocal(gm[:, 4], gm[:, 3]))
            then(dve.tensor_tensor(gm[:, 5, 0, :], gm[:, 4, 0, :], gm[:, 4, 1, :], ALU.add))
            then(dve.tensor_scalar(gm[:, 5, 0, :], gm[:, 5, 0, :], 1e-10, None, ALU.add))
            then(dve.reciprocal(gm[:, 5, 1, :], gm[:, 5, 0, :]))
            for k in range(2):
                then(dve.tensor_tensor(gm[:, 6, k, :], gm[:, 4, k, :], gm[:, 5, 1, :], ALU.mult))

            dve.tensor_tensor(chosen[:, :, :].rearrange("p e n -> p n e"), gt[:, 1], gt[:, 2], ALU.add).then_inc(chosen_ready, 1)
            dve.wait_ge(ranks_ps, 1)
            per_tile = ps[:, 7, 0:NE * NT].rearrange("p (e n) -> p e n", e=NE)
            in_tile = ps[:, 6, 0:NE * NT].rearrange("p (e n) -> p e n", e=NE)
            flat = slot_map[:, 0].rearrange("p e n -> p (e n)")
            then(dve.tensor_copy(slot_map[:, 2], per_tile))
            then(dve.tensor_tensor_scan(flat, ones_f[:, :], slot_map[:, 2].rearrange("p e n -> p (e n)"), 0.0, ALU.mult, ALU.add))
            then(dve.tensor_tensor(slot_map[:, 1], slot_map[:, 0], slot_map[:, 2], ALU.subtract))
            first = slot_map[:, 1, :, 0:1].rearrange("p e n -> p (e n)")
            last = slot_map[:, 0, :, NT - 1:NT].rearrange("p e n -> p (e n)")
            then(dve.tensor_tensor(counts[:, 0, :], last, first, ALU.subtract))
            dve.wait_ge(steps_ready, 1)
            then(dve.tensor_copy(steps[:, :], steps_i[:, :]))
            then(dve.tensor_scalar(counts[:, 1, :], counts[:, 0, :], 1.0 / P, None, ALU.mult))
            then(dve.tensor_tensor(over[:, :, :], counts[:, 1, :].rearrange("p (e a) -> p e a", a=1).broadcast_to([P, NE, NT]),
                                   steps[:, 0:NT].rearrange("p (a n) -> p a n", a=1).broadcast_to([P, NE, NT]), ALU.is_gt))
            then(dve.tensor_reduce(counts[:, 2, :], over[:, :, :], AX.X, ALU.add))
            then(dve.tensor_tensor_scan(counts[:, 3, :], ones_f[:, 0:NE], counts[:, 2, :], 0.0, ALU.mult, ALU.add))
            then(dve.tensor_tensor(counts[:, 4, :], counts[:, 3, :], counts[:, 2, :], ALU.subtract))
            then(dve.scalar_tensor_tensor(counts[:, 5, :], counts[:, 4, :], float(P), first, ALU.mult, ALU.subtract))
            then(dve.tensor_tensor(slot_map[:, 1], slot_map[:, 1],
                                   counts[:, 5, :].rearrange("p (e a) -> p e a", a=1).broadcast_to([P, NE, NT]), ALU.add))
            then(dve.tensor_tensor(slot_map[:, 1], slot_map[:, 1], in_tile, ALU.add))
            for k in range(2):
                then(dve.tensor_tensor(gt[:, 3], gt[:, 1 + k], slot_map[:, 1].rearrange("p e n -> p n e"), ALU.mult))
                then(dve.tensor_reduce(slot_f[:, k, :], gt[:, 3], AX.X, ALU.add))
            then(dve.tensor_copy(slot[:, :, :], slot_f[:, :, :]))
            then(dve.tensor_tensor(tile_e[:, :, 0:NE - 1],
                                   counts[:, 3, 0:NE - 1].rearrange("p (a e) -> p a e", a=1).broadcast_to([P, TILES, NE - 1]),
                                   steps[:, :].rearrange("p (t a) -> p t a", a=1).broadcast_to([P, TILES, NE - 1]), ALU.is_le))
            then(dve.tensor_reduce(tile_f[:, :], tile_e[:, :, 0:NE - 1], AX.X, ALU.add))
            dve.tensor_copy(tile_expert[:, :], tile_f[:, :]).then_inc(routed, 1)

            def maxima(i, c, kt, reused=True):
                n = 6 * i + c
                if kt == 0 and reused:
                    dve.wait_ge(m_T, n - 1)
                for r in (2 * kt, 2 * kt + 1):
                    dve.wait_ge(x_ready, 16 * n + r + 1)
                    dve.tensor_reduce(mneg[:, c % 2, r:r + 1], ps[:, 2 + 2 * (r % 2):4 + 2 * (r % 2), :], AX.XY, ALU.max,
                                      negate=True).then_inc(max_done, 1)

            def split_max(i, c, reused):
                n, k = 6 * i + c, c % 2
                src = ps[0:HG * TPC, 7, 0:P]
                dve.wait_ge(m_T, n + 1)
                if reused:
                    dve.wait_ge(m_stored, 16 * n - 16)
                dve.tensor_copy(m_parts[:, k, 0], src).then_inc(m_hi, 1)
                dve.wait_ge(m_hi, n + 1)
                dve.tensor_tensor(m_rest[:, 0], src, m_parts[:, k, 0], ALU.subtract).then_inc(m_read, 1)
                dve.wait_ge(m_read, n + 1)
                dve.tensor_copy(m_parts[:, k, 1], m_rest[:, 0]).then_inc(m_mid, 1)
                dve.wait_ge(m_mid, n + 1)
                dve.tensor_tensor(m_rest[:, 1], m_rest[:, 0], m_parts[:, k, 1], ALU.subtract).then_inc(m_rest2, 1)
                dve.wait_ge(m_rest2, n + 1)
                dve.tensor_copy(m_parts[:, k, 2], m_rest[:, 1]).then_inc(m_split, 1)

            def divide(i, c):
                n = 6 * i + c
                o = ps[:, 7, :].rearrange("p (a c) -> p a c", c=32)
                dve.wait_ge(o_T, n + 1)
                dve.reciprocal(recip[:, c % 2, :], o[:, :, D:D + 1].rearrange("p a c -> p (a c)")).then_inc(recip_ready, 1)
                dve.wait_ge(recip_ready, n + 1)
                dve.tensor_tensor(attn_all[:, bass.ds(n, 1), :, :].rearrange("p n q (h d) -> p (n q h) d", d=D),
                                  o[:, :, 0:D],
                                  recip[:, c % 2, :].rearrange("p (a c) -> p a c", c=1).broadcast_to([P, HG * TPC, D]),
                                  ALU.mult).then_inc(attn_ready, 1)

            for c in range(2):
                for kt in range(KT):
                    maxima(0, c, kt, False)
                if c == 0:
                    for s in range(2):
                        dve.wait_ge(v_ready[s], NC // 2)
                    for g in range(NBUF):
                        fill_v(g, g)
            split_max(0, 0, False)

            def step(i, c, n):
                if c % 2 == 0 and c >= 2 and (n is None or n + 4 < NH):
                    dve.wait_ge(pv_done, 2 * KT * group(i, c))
                    fill_v(group(i, c + 4), buf(c + 4))
                if n is None and c == 4:
                    dve.wait_ge(split_late[0], NC - 2)
                for kt in range(KT):
                    if n is None or n + 2 < NH:
                        maxima(i, c + 2, kt)
                    if kt == 3 and (n is None or n + 1 < NH):
                        split_max(i, c + 1, n is None or n >= 1)
                    if kt == 6 and (n is None or n >= 1):
                        divide(i, c - 1)

            def experts():
                def tile(i, k):
                    s = k % 2
                    if exists(i, k + 2):
                        take(i, k + 2)
                    dve.wait_ge(silu_ready[s], used(i, k) + 1)
                    dve.tensor_tensor(hid[:, s, :], silu[:, s, :], ps[:, s, F:2 * F], ALU.mult).then_inc(hid_ready[s], 1)
                    if exists(i, k - 2):
                        give(i, k - 2)

                def take(i, k):
                    s = k % 2
                    dve.wait_ge(xg_T[k % 4], used(i, k, 4) + 1)
                    dve.tensor_copy(xgT[:, s, :], ps[:, 7, 0:P]).then_inc(xgT_ready[s], 1)

                def give(i, k):
                    s = k % 2
                    dve.wait_ge(down_done[s], used(i, k) + 1)
                    past(dve, result_out[s], used(i, k), 16)
                    dve.tensor_copy(result[:, s, :], ps[:, 4 + s, 0:E]).then_inc(result_ready[s], 1)
                take(0, 0)
                take(0, 1)
                over_tiles(dve, tile)
                give(TILES // 4 - 1, 2)
                give(TILES // 4 - 1, 3)
            over_halves(dve, step, experts)
            divide(0, NH - 1)

            dve.wait_ge(attn_ready, NH)

            def pair(i):
                for s in range(2):
                    past(dve, a_T[s], i)
                    for q in range(TPC):
                        ins = dve.tensor_scalar(late_tile(s, 0)[:, q * E:(q + 1) * E].rearrange("p (g c) -> p g c", g=HG),
                                              qk_f[:, 0, :].rearrange("p (b g a q c) -> p b a q g c", b=B, g=HG, a=2, q=TPC)
                                              [:, bass.ds(i, 1), s, q].rearrange("p b g c -> p (b g) c"), 1.0, None, ALU.mult)
                    ins.then_inc(a_staged[s], 1)
                    dve.wait_ge(x2_in[s], 16 * i + 16)
                    past(dve, y_ready[s], i)
                    dve.tensor_tensor(late_tile(s, 2).rearrange("p (q e) -> p q e", e=E),
                                      late_tile(s, 3).rearrange("p (q e) -> p q e", e=E),
                                      x_all[:, bass.ds((2 * i + s) * TPC, TPC), :], ALU.add).then_inc(a_sum[s], 1)
                for s in range(2):
                    dve.wait_ge(a_proj[s], i + 1)
                    dve.wait_ge(a_sum[s], i + 1)
                    past(dve, y_out[s], i, 16)
                    dve.tensor_tensor(late_tile(2, s), ps[:, 2 + s, :], late_tile(s, 2), ALU.add).then_inc(y_ready[s], 1)
            dve.wait_ge(mixed_step, 4)
            over_pairs(dve, pair)

        @block.tensor
        def _(pe):
            pe.wait_ge(ident_step, 2)
            pe.wait_ge(small_in, 16 * 5)
            pe.transpose(ps[:, 6, 0:NE], rw_in[:, :], ident[0:NE, 0:NE]).then_inc(rw_T, 1)
            pe.wait_ge(const_step, NE + 4)
            pe.transpose(ps[:, 7, 0:2], b_in[:, 1, :], ident[0:2, 0:2]).then_inc(bias_T, 1)
            pe.wait_ge(rw_ready, 1)
            pe.wait_ge(proj_in, 64)

            def turn_norm(i, s):
                pe.wait_ge(xn_ready[s], i + 1)
                past(pe, xnT_kept[s], i)
                for j in range(TPC):
                    mm = pe.transpose(ps[:, s, j * P:(j + 1) * P], xn[:, s, j, :], ident[:, :])
                mm.then_inc(xn_T[s], 1)

            def project(i, s, xnT):
                for z in range(2):
                    past(pe, qk_ready[z], 2 * i + s)
                    pe.matmul(ps[:, 6 + z, :], wqk[:, z, :], xnT, start=True, stop=True).then_inc(qk_ps[z], 1)

            def pair(i):
                for s in range(2):
                    if s == 0:
                        turn_norm(i, 1)
                    elif type(i) is not int or i < NC // 2 - 1:
                        turn_norm(i + 1, 0)
                    pe.wait_ge(xnT_ready[s], i + 1)
                    past(pe, lg_ready[s], i)
                    past(pe, v_ready[s], i)
                    for j in range(TPC):
                        mm = pe.matmul(v_lg[:, s, j // 2, j % 2], xnT_st[:, s, j * P:(j + 1) * P], wvr[:, :],
                                       start=True, stop=True)
                    mm.then_inc(v_ps[s], 1)
                    if type(i) is int and i == 0:
                        if s == 0:
                            pe.wait_ge(const_step, NE + 5)
                        project(0, s, xnT_st[:, s, :])
            turn_norm(0, 0)
            over_pairs(pe, pair)
            for s in range(2):
                pe.wait_ge(xnT_kept[s], NC // 2)
            with pe.Fori(1, NC // 2) as i:
                for s in range(2):
                    project(i, s, xnT_all[:, bass.ds((2 * i + s) * CH, CH)])
            pe.wait_ge(chosen_ready, 1)
            pe.wait_ge(before_step, 2)
            for z in range(2):
                pe.wait_ge(qk_ready[z], NC)
            pe.matmul(ps[:, 6, 0:NE * NT], before[:, :], chosen[:, :, :].rearrange("p e n -> p (e n)"), start=True, stop=True)
            pe.matmul(ps[:, 7, 0:NE * NT], ones[:, :], chosen[:, :, :].rearrange("p e n -> p (e n)"),
                      start=True, stop=True).then_inc(ranks_ps, 1)

            for s in range(2):
                pe.wait_ge(v_ready[s], NC // 2)
            pe.wait_ge(routed, 1)
            pe.wait_ge(rows_const, 2 * NBUF)
            pe.wait_ge(vx_const, NBUF)

            def maxima(i, c, r):
                n, s = 6 * i + c, buf(c)
                if r == 0 and c % 2 == 0:
                    pe.wait_ge(qk_in[s], LOADS * (turn(i, c) + 1))
                h, q = r // TPC, r % TPC
                if c >= 1 or r >= 2:
                    pe.wait_ge(max_done, 16 * n + r - 1)
                for half in range(2):
                    mm = pe.matmul(ps[:, 2 + 2 * (r % 2) + half, :], q_sb[s][0:KX, c % 2, h, q * P:(q + 1) * P],
                                   k_sb[s][0:KX, half, h, :], start=True, stop=True)
                mm.then_inc(x_ready, 1)

            def turn_max(i, c, first):
                n = 6 * i + c
                pe.wait_ge(max_done, 16 * n + 16)
                if not first:
                    pe.wait_ge(attn_ready, n - 2)
                pe.transpose(ps[0:HG * TPC, 7, 0:P], mneg[:, c % 2, :], ident[:, :]).then_inc(m_T, 1)

            def turn_output(i, c):
                n = 6 * i + c
                pe.wait_ge(o_out, n + 1)
                if type(n) is int and n >= NH - 2:
                    pe.wait_ge(attn_ready, n)
                else:
                    pe.wait_ge(m_read, n + 3)
                for q in range(TPC):
                    mm = pe.transpose(ps[:, 7, q * P:(q + 1) * P], oT[:, c % 2, q * P:(q + 1) * P], ident[:, :])
                mm.then_inc(o_T, 1)

            def scores(i, c, kt, h, first):
                n, s = 6 * i + c, buf(c)
                if kt == 0 and h == 0:
                    pe.wait_ge(m_in, 16 * n + 16)
                if not first:
                    pe.wait_ge(exp_done, 4 * (KT * n + kt) + h - 1)
                pe.matmul(ps[:, h % 2, :], k_sb[s][0:KS, kt // 4, h, kt % 4 * P:(kt % 4 + 1) * P],
                          q_sb[s][0:KS, c % 2, h, :], start=True, stop=True).then_inc(scores_ready, 1)

            def weigh(i, c, kt, half):
                n, s = 6 * i + c, buf(c)
                if half == 0:
                    pe.wait_ge(exp_done, 4 * (KT * n + kt) + 4)
                if kt == 0 and half == 0:
                    if c >= 1:
                        pe.wait_ge(o_out, n)
                    if c % 2 == 0:
                        pe.wait_ge(vx_ready, group(i, c) + 1)
                for h in range(HG):
                    mm = pe.matmul(ps[32 * h:32 * h + 32, 6, half * CH // 2:(half + 1) * CH // 2], vx[s][:, kt, h, :],
                                   probs[:, kt % 2, h, half * CH // 2:(half + 1) * CH // 2],
                                   start=(kt == 0 and half == 0), stop=(kt == KT - 1 and half == 1))
                if half == 1:
                    mm.then_inc(pv_done, 1)

            for c in range(2):
                for kt in range(KT):
                    for r in (2 * kt, 2 * kt + 1):
                        maxima(0, c, r)
            turn_max(0, 0, True)

            def weigh_before(i, c, kt, half, n):
                if kt >= 1:
                    weigh(i, c, kt - 1, half)
                elif n is None or n >= 1:
                    weigh(i, c - 1, KT - 1, half)

            def step(i, c, n):
                for kt in range(KT):
                    scores(i, c, kt, 0, n == 0 and kt == 0)
                    if n is None or n + 2 < NH:
                        maxima(i, c + 2, 2 * kt)
                    scores(i, c, kt, 1, n == 0 and kt == 0)
                    weigh_before(i, c, kt, 0, n)
                    scores(i, c, kt, 2, False)
                    if n is None or n + 2 < NH:
                        maxima(i, c + 2, 2 * kt + 1)
                    scores(i, c, kt, 3, False)
                    weigh_before(i, c, kt, 1, n)
                    if kt == 2 and (n is None or n + 1 < NH):
                        turn_max(i, c + 1, n is not None and n < 2)
                    if kt == 5 and (n is None or n >= 1):
                        turn_output(i, c - 1)

            def experts():
                pe.wait_ge(ffn_in, 16 * (2 * NE + 1))
                pe.wait_ge(exp_done, 4 * KT * BREAK)
                pe.wait_ge(max_done, 16 * (BREAK + 2))
                pe.wait_ge(attn_ready, BREAK - 1)
                pe.wait_ge(m_read, BREAK + 1)

                def expert(i, k):
                    return nc.values_load(tile_expert[0:1, bass.ds(4 * i + k, 1)], engines=[mybir.EngineType.PE],
                                          min_val=0, max_val=NE - 1,
                                          skip_runtime_bounds_check_because="it counts how many of seven ends are passed")

                def take(i, k):
                    pe.wait_ge(xg_in[k % 4], 16 * (used(i, k, 4) + 1))
                    if exists(i, k - 1):
                        pe.wait_ge(xgT_ready[(k - 1) % 2], used(i, k - 1) + 1)
                    pe.transpose(ps[:, 7, 0:P], xg[:, k % 4, :], ident[:, :]).then_inc(xg_T[k % 4], 1)

                def turn_hidden(i, k):
                    s = k % 2
                    pe.wait_ge(hid_ready[s], used(i, k) + 1)
                    for f in range(F // P):
                        mm = pe.transpose(ps[:, 2 + s, f * P:(f + 1) * P], hid[:, s, f * P:(f + 1) * P], ident[:, :])
                    mm.then_inc(hid_T[s], 1)

                def down(i, k):
                    s, e = k % 2, expert(i, k)
                    pe.wait_ge(hidT_ready[s], used(i, k) + 1)
                    for f in range(F // P):
                        mm = pe.matmul(ps[:, 4 + s, 0:E], hidT[:, s, f * P:(f + 1) * P],
                                       w_dn[:, bass.ds(e, 1), f].rearrange("p e d -> p (e d)"),
                                       start=(f == 0), stop=(f == F // P - 1))
                    mm.then_inc(down_done[s], 1)

                def tile(i, k):
                    s, e = k % 2, expert(i, k)
                    pe.wait_ge(xgT_ready[s], used(i, k) + 1)
                    pe.matmul(ps[:, s, :], xgT[:, s, :], w_gu[:, bass.ds(e, 1)].rearrange("p e a f -> p (e a f)"),
                              start=True, stop=True).then_inc(gu_ready[s], 1)
                    if exists(i, k + 2):
                        take(i, k + 2)
                    if exists(i, k - 1):
                        turn_hidden(i, k - 1)
                    if exists(i, k - 2):
                        down(i, k - 2)
                take(0, 0)
                take(0, 1)
                over_tiles(pe, tile)
                turn_hidden(TILES // 4 - 1, 3)
                down(TILES // 4 - 1, 2)
                pe.wait_ge(result_ready[1], TILES // 2 - 1)
                down(TILES // 4 - 1, 3)
                for s in range(2):
                    pe.wait_ge(result_ready[s], TILES // 2)
            over_halves(pe, step, experts)
            weigh(0, NH - 1, KT - 1, 0)
            weigh(0, NH - 1, KT - 1, 1)
            turn_output(0, NH - 1)

            def pair(i):
                for s in range(2):
                    pe.wait_ge(a_staged[s], i + 1)
                    past(pe, a_sb[s], i)
                    for q in range(TPC):
                        mm = pe.transpose(ps[:, s, q * P:(q + 1) * P], late_tile(s, 0)[:, q * P:(q + 1) * P], ident[:, :])
                    mm.then_inc(a_T[s], 1)
                for s in range(2):
                    pe.wait_ge(a_sb[s], i + 1)
                    past(pe, y_ready[s], i)
                    for q in range(TPC):
                        mm = pe.matmul(ps[:, 2 + s, q * E:(q + 1) * E], late_tile(s, 1)[:, q * P:(q + 1) * P], wo[:, :],
                                       start=True, stop=True)
                    mm.then_inc(a_proj[s], 1)
            over_pairs(pe, pair)


_INS = ["L0_attn_inputs", "L0_attn_Wq", "L0_attn_bq", "L0_attn_Wk", "L0_attn_bk", "L0_attn_Wv", "L0_attn_bv",
        "L0_attn_Wo", "L0_attn_bo", "L0_ffn_router_w", "L0_ffn_w_gate", "L0_ffn_w_up", "L0_ffn_w_down"]


def kernel(**inputs):
    import concourse.bacc as bacc
    from concourse.bass_utils import run_bass_kernel_spmd

    nc = bacc.Bacc("TRN2", target_bir_lowering=False, num_devices=1)
    arrays, args = {}, []
    for name in _INS:
        a = np.ascontiguousarray(inputs[name])
        arrays[name] = a
        args.append(nc.dram_tensor(name, a.shape, mybir.dt.from_np(a.dtype), kind="ExternalInput").ap())
    y = nc.dram_tensor("y", (B, S, E), F32, kind="ExternalOutput").ap()
    build(nc, *args, y)
    return run_bass_kernel_spmd(nc, [arrays], core_ids=[0]).results[0]["y"]
```

```python
from contextlib import ExitStack

import numpy as np
import concourse.bass as bass
from concourse import mybir

F32 = mybir.dt.float32
BF16 = mybir.dt.bfloat16
ALU = mybir.AluOpType
ACT = mybir.ActivationFunctionType
AX = mybir.AxisListType

P = 128
B, S, E = 4, 1024, 128
H = 16
D = E // H
NE = 8
F = 256
T = B * S
NT = T // P
CH = 512
NC = T // CH
TPC = CH // P
HG = 4
NG = B * H // HG
NH = 2 * NG
KT = S // P
PARTS = 3
ROWS = PARTS * PARTS * D
SHIFT = 96
KX = SHIFT
assert ROWS <= SHIFT
KS = SHIFT + PARTS
NBUF = 3
SCALE = float(np.float32(1.0) / np.sqrt(np.float32(D)))
EPS = 1e-5
BIG = 1.7e38
TWO_ONES = float(np.array([0x3F803F80], np.uint32).view(np.float32)[0])
TILES = 2 * NT + NE
EARLY = NC - 2
BREAK = NH - 6
AHEAD = 9
FIRST_MAXIMA = np.array_split([(c, r) for c in (1, 2) for r in range(2 * KT)][AHEAD:], 2 * KT)
FIRST_MAXIMA = [[(int(c), int(r)) for c, r in part] for part in FIRST_MAXIMA]
LOADS = 16 * (PARTS + PARTS * PARTS)


def build(nc, x, Wq, bq, Wk, bk, Wv, bv, Wo, bo, router_w, w_gate, w_up, w_down, out):
    ctx = ExitStack()
    with ctx:
        ctx.enter_context(nc.allow_non_contiguous_dma(reason="bias columns"))

        def sb(name, shape, dt=F32):
            return ctx.enter_context(nc.sbuf_tensor(name, shape, dt))

        def sem(name):
            return ctx.enter_context(nc.semaphore(name))

        def dram(name, shape, dt):
            return nc.dram_tensor(name, shape, dt).ap()

        def group(i, c):
            return 3 * i + c // 2

        def buf(c):
            return (c // 2) % NBUF

        def turn(i, c):
            return i + c // 2 // NBUF

        parts_dram = [dram(f"{z}_parts", [B, HG, 2, PARTS, D * HG, CH], BF16) for z in "qk"]
        slots_dram = dram("slots", [TILES * P, E], F32)
        results_dram = dram("results", [TILES * P, E], F32)
        shift_dram = dram("shift", [2, PARTS, HG * TPC, P], BF16)

        x_sb = sb("x_sb", [P, T])
        x_all = x_sb[:, :].rearrange("p (n e) -> p n e", e=E)
        qk_f = sb("qk_f", [P, 2, T])
        attn_all = qk_f[:, 0, :].rearrange("p (n q c) -> p n q c", n=NH, q=TPC)
        picked = [x_all, qk_f[:, 1, :].rearrange("p (n e) -> p n e", e=E)]
        v_all = sb("v_all", [P, B, HG, KT, HG * D])
        w_gu = sb("w_gu", [P, NE, 2, F])
        xnT_all = w_gu[:, :, :, :].rearrange("p e a f -> p (e a f)")
        w_dn = sb("w_dn", [P, NE, F // P, E])
        probs = sb("probs", [P, 2, HG, CH])
        early = probs[:, :, :, :].rearrange("p u h q -> p (u h q)")
        gt = early[:, 0:6 * NT * NE].rearrange("p (k n e) -> p k n e", k=6, e=NE)
        slot_map = early[:, 6 * NT * NE:10 * NT * NE].rearrange("p (k e n) -> p k e n", k=4, e=NE)
        wq_in, wk_in, wo = (sb(n, [P, E]) for n in ("wq_in", "wk_in", "wo"))
        wvr = sb("wvr", [P, E + NE])
        wqk = sb("wqk", [P, 2, E])
        bqk = sb("bqk", [P, 2])
        b_in = sb("b_in", [2, 2, E])
        bo_row = sb("bo_row", [P, E])
        bv_all = sb("bv_all", [P, B, E])
        rw_in = sb("rw_in", [NE, E])
        ident = sb("ident", [P, P])
        rank = sb("rank", [P, NE])
        before = sb("before", [P, P], BF16)
        ones = sb("ones", [P, P], BF16)
        ones_f = sb("ones_f", [P, NE * NT])
        steps_i = sb("steps_i", [P, TILES], mybir.dt.int32)
        steps = sb("steps", [P, TILES])
        stats = sb("stats", [P, NT, 6])
        mom = sb("mom", [P, 5, NT])
        lg = sb("lg", [P, NT, NE])
        gm = sb("gm", [P, 8, 2, NT])
        chosen = sb("chosen", [P, NE, NT], BF16)
        counts = sb("counts", [P, 6, NE])
        over = early[:, 10 * NT * NE:11 * NT * NE].rearrange("p (e n) -> p e n", e=NE)
        tile_e = early[:, 11 * NT * NE:(11 * NT + TILES) * NE].rearrange("p (t e) -> p t e", e=NE)
        tile_f = sb("tile_f", [P, TILES])
        tile_expert = sb("tile_expert", [P, TILES], mybir.dt.int32)
        slot_f = sb("slot_f", [P, 2, NT])
        slot = sb("slot", [P, 2, NT], mybir.dt.uint32)
        shared = sb("shared", [P, 2560])
        xn = shared[:, 0:1024].rearrange("p (s j e) -> p s j e", s=2, e=E)
        xnT_st = shared[:, 1024:2048].rearrange("p (s t) -> p s t", s=2)
        zeros = shared[:, 0:1024]
        xg = shared[:, 0:512].rearrange("p (s e) -> p s e", s=4)
        xgT = shared[:, 512:768].rearrange("p (s e) -> p s e", s=2)
        silu = shared[:, 768:1280].rearrange("p (s f) -> p s f", s=2)
        hid = shared[:, 1280:1792].rearrange("p (s f) -> p s f", s=2)
        hidT = shared[:, 1792:2304].rearrange("p (s f) -> p s f", s=2)
        result = shared[:, 2304:2560].rearrange("p (s e) -> p s e", s=2)
        rest = sb("rest", [P, 2, CH])
        part = sb("part", [P, 2, PARTS, CH], BF16)
        part_1 = w_dn[:, :, :, :].rearrange("p e k d -> p (e k d)").bitcast(BF16)[:, 0:2 * PARTS * CH] \
            .rearrange("p (z k t) -> p z k t", z=2, k=PARTS)

        def part_of(c):
            return part_1 if c == 1 else part[:, :, :, :]

        qk_buf = sb("qk_buf", [P, NBUF, 2, 2, HG, CH], BF16)
        q_sb = [qk_buf[:, s, 0] for s in range(NBUF)]
        k_sb = [qk_buf[:, s, 1] for s in range(NBUF)]
        vx = [sb(f"vx{s}", [P, KT, HG, 32]) for s in range(NBUF)]
        mneg = sb("mneg", [P, 2, HG * TPC])
        m_parts = sb("m_parts", [HG * TPC, 2, PARTS, P], BF16)
        m_rest = sb("m_rest", [HG * TPC, 2, P])
        oT = sb("oT", [P, 2, CH])
        recip = sb("recip", [P, 2, HG * TPC])
        assert buf(NH - 1) == 0
        late = [qk_buf[:, s].rearrange("p z a h q -> p (z a h q)").bitcast(F32)
                .rearrange("p (k t) -> p k t", t=CH) for s in (1, 2)]

        def staged_tile(c):
            return late[0][:, c % 2]

        def attn_T(c):
            return late[0][:, 2 + c] if c < EARLY else late[1][:, c - EARLY]

        def y_tile(c):
            return late[1][:, 2 + c] if c < 6 else late[0][:, 2 + c - 6]

        ps = ctx.enter_context(nc.psum_tensor("ps", [P, 8, CH], F32))
        v_lg = ps[:, 2:6, 0:2 * (E + NE)].rearrange("p (s b) (j e) -> p s b j e", s=2, j=2)

        x_t = x.rearrange("b (m p) e -> p (b m) e", p=P)
        out_c = out.rearrange("b (a q p) e -> (b a) p q e", a=2, q=TPC)

        def sems(name, n=2):
            return [sem(f"{name}{k}") for k in range(n)]

        x_in, proj_in, small_in, ffn_in = sems("x_in", 4), sem("proj_in"), sem("small_in"), sem("ffn_in")
        ident_step, const_step, stat_done, mom_step = (sem(n) for n in ("ident_step", "const_step", "stat_done", "mom_step"))
        var_ready, std_ready, rw_T, rw_ready = (sem(n) for n in ("var_ready", "std_ready", "rw_T", "rw_ready"))
        xn_kept, xnT_kept, lg_ready = (sems(n) for n in ("xn_kept", "xnT_kept", "lg_ready"))
        bias_T = sem("bias_T")
        xn_ready, xn_T, xnT_ready, v_ps, v_ready = (sems(n) for n in ("xn_ready", "xn_T", "xnT_ready", "v_ps", "v_ready"))
        qk_ps, qk_ready, split_step, part_ready = sems("qk_ps"), sems("qk_ready"), sems("split_step"), sems("part_ready")
        split_late, first_stored, late_stored, qk_in = sems("split_late"), sems("first_stored"), sems("late_stored"), sems("qk_in", NBUF)
        gexp_in, gexp_out, chosen_ready, ranks_ps = (sem(n) for n in ("gexp_in", "gexp_out", "chosen_ready", "ranks_ps"))
        zeros_ready, zeros_stored, steps_ready, before_step = (sem(n) for n in (
            "zeros_ready", "zeros_stored", "steps_ready", "before_step"))
        routed, scattered, picked_in, mixed_step = (sem(n) for n in ("routed", "scattered", "picked_in", "mixed_step"))
        rows_const, vx_const, vx_ready = sem("rows_const"), sem("vx_const"), sem("vx_ready")
        gates_ready, residual_in = sem("gates_ready"), sem("residual_in")
        scores_ready, exp_done, pv_done = sem("scores_ready"), sem("exp_done"), sem("pv_done")
        x_ready, max_done, m_T = (sem(n) for n in ("x_ready", "max_done", "m_T"))
        m_hi, m_read, m_mid, m_rest2, m_split = (sem(n) for n in ("m_hi", "m_read", "m_mid", "m_rest2", "m_split"))
        m_stored, m_in = sem("m_stored"), sem("m_in")
        o_out, o_T, recip_ready, attn_ready = (sem(n) for n in ("o_out", "o_T", "recip_ready", "attn_ready"))
        xg_in, xg_T = sems("xg_in", 4), sems("xg_T", 4)
        xgT_ready, gu_ready, silu_ready, hid_ready, hid_T, hidT_ready, down_done, result_ready, result_out = (
            sems(n) for n in ("xgT_ready", "gu_ready", "silu_ready", "hid_ready", "hid_T", "hidT_ready", "down_done",
                              "result_ready", "result_out"))
        a_staged, a_T, a_sb, a_proj, y_ready = (sem(n) for n in ("a_staged", "a_T", "a_sb", "a_proj", "y_ready"))
        y_out = sem("y_out")

        def past(eng, s, k, unit=1):
            if type(k) is not int or k > 0:
                eng.wait_ge(s, unit * k)

        def over_pairs(eng, pair):
            pair(0)
            with eng.Fori(1, NC // 2 - 1) as i:
                pair(i)
            pair(NC // 2 - 1)

        def over_tiles(eng, tile):
            for k in range(4):
                tile(0, k)
            with eng.Fori(1, TILES // 4 - 1) as i:
                for k in range(4):
                    tile(i, k)
            for k in range(4):
                tile(TILES // 4 - 1, k)

        def exists(i, k):
            return type(i) is not int or 0 <= 4 * i + k < TILES

        def used(i, k, slots=2):
            return 4 // slots * i + k // slots

        def score_bank(c, h):
            return {NH - 2: (0, 1, 4, 5), NH - 1: (0, 1, 2, 3)}.get(c, (0, 1, 0, 1))[h]

        def over_halves(eng, step, experts=None):
            for c in range(2):
                step(0, c, c)
            with eng.Fori(0, (BREAK - 2) // 6) as i:
                for c in range(2, 8):
                    step(i, c, None)
            if experts:
                experts()
            for c in range(BREAK, NH):
                step(0, c, c)

        block = ctx.enter_context(nc.Block())

        @block.sync
        def _(sp):
            for k in range(4):
                n = NT // 4
                sp.dma_start(x_all[:, k * n:(k + 1) * n, :], x_t[:, k * n:(k + 1) * n, :]).then_inc(x_in[k], 16)
            sp.dma_start(rw_in[:, :], router_w).then_inc(small_in, 16)
            sp.dma_start(b_in[0:1, 0, :], bq.rearrange("(a e) -> a e", a=1)).then_inc(small_in, 16)
            sp.dma_start(b_in[1:2, 0, :], bk.rearrange("(a e) -> a e", a=1)).then_inc(small_in, 16)
            sp.dma_start(wvr[:, 0:E], Wv).then_inc(proj_in, 16)
            sp.dma_start(wq_in[:, :], Wq).then_inc(proj_in, 16)
            sp.dma_start(wk_in[:, :], Wk).then_inc(proj_in, 16)
            sp.dma_start(wo[:, :], Wo).then_inc(proj_in, 16)
            sp.dma_start(bv_all[:, :, :], bv.rearrange("(a b e) -> a b e", a=1, b=1).broadcast_to([P, B, E])).then_inc(small_in, 16)
            sp.dma_start(bo_row[:, :], bo.rearrange("(a e) -> a e", a=1).broadcast_to([P, E])).then_inc(small_in, 16)

            for c in range(2):
                for z in range(2):
                    sp.wait_ge(part_ready[z], c + 1)
                    for k in range(PARTS):
                        sp.dma_start(parts_dram[z][0, :, c, k], part_of(c)[:, z, k]).then_inc(first_stored[z], 16)
            for z in range(2):
                sp.wait_ge(first_stored[z], 16 * 2 * PARTS)

            def load_group(g, s):
                k_src = parts_dram[1].rearrange("b g a k (d h) t -> (b g) (k d) a (h t)", h=HG)[bass.ds(g, 1)] \
                    .rearrange("g r a t -> (g r) a t")
                for copy in range(PARTS):
                    r = copy * PARTS * D
                    sp.dma_start(k_sb[s][r:r + PARTS * D].rearrange("r a h t -> r a (h t)"), k_src).then_inc(qk_in[s], 16)
                for part in range(PARTS):
                    q_src = parts_dram[0].rearrange("b g a k (d h) t -> (b g) k d a (h t)", h=HG)[bass.ds(g, 1), part] \
                        .rearrange("g r a t -> (g r) a t")
                    for copy in range(PARTS):
                        r = (part * PARTS + copy) * D
                        sp.dma_start(q_sb[s][r:r + D].rearrange("r a h t -> r a (h t)"), q_src).then_inc(qk_in[s], 16)

            sp.wait_ge(rows_const, 2 * NBUF)
            for g in range(NBUF):
                load_group(g, g)

            def shift_rows(i, c):
                n = 6 * i + c
                sp.wait_ge(m_split, n + 1)
                sp.dma_start(shift_dram[c % 2].rearrange("k a t -> a k t"), m_parts[:, c % 2]).then_inc(m_stored, 16)
                sp.wait_ge(m_stored, 16 * n + 16)
                sp.dma_start(q_sb[buf(c)][SHIFT:SHIFT + PARTS, c % 2].rearrange("r h q -> r (h q)"),
                               shift_dram[c % 2].rearrange("k a t -> k (a t)")).then_inc(m_in, 16)

            sp.wait_ge(qk_in[0], LOADS)
            shift_rows(0, 0)
            for z in range(2):
                sp.wait_ge(qk_ready[z], NC)
            for e in range(NE):
                sp.dma_start(w_gu[:, e, 0, :], w_gate[e]).then_inc(ffn_in, 16)
                sp.dma_start(w_gu[:, e, 1, :], w_up[e]).then_inc(ffn_in, 16)
            sp.dma_start(w_dn[:, :, :, :].rearrange("p e k d -> p (e k) d"),
                         w_down.rearrange("e (k p) d -> p (e k) d", p=P)).then_inc(ffn_in, 16)

            def step(i, c, n):
                if c % 2 == 0 and c >= 2 and (n is None or n + 4 < NH):
                    if c >= 4:
                        for z in range(2):
                            sp.wait_ge(late_stored[z], 16 * PARTS * (NC - 2))
                    sp.wait_ge(scores_ready, 8 * KT * group(i, c))
                    load_group(group(i, c + 4), buf(c + 4))
                if n is None or n + 1 < NH:
                    shift_rows(i, c + 1)

            def experts():
                def load(i, k):
                    sp.dma_start(xg[:, k % 4, :], slots_dram[bass.ds((4 * i + k) * P, P), :]).then_inc(xg_in[k % 4], 16)

                def tile(i, k):
                    if exists(i, k + 4):
                        sp.wait_ge(xg_T[k], used(i, k, 4) + 1)
                        load(i, k + 4)
                    if exists(i, k - 4):
                        store(i, k - 4)

                def store(i, k):
                    sp.wait_ge(result_ready[k % 2], used(i, k) + 1)
                    sp.dma_start(results_dram[bass.ds((4 * i + k) * P, P), :], result[:, k % 2, :]).then_inc(result_out[k % 2], 16)
                sp.wait_ge(scattered, 16 * 2 * NT)
                for k in range(4):
                    load(0, k)
                over_tiles(sp, tile)
                for k in range(4):
                    store(TILES // 4 - 1, k)
            over_halves(sp, step, experts)

            for c in range(NC):
                sp.wait_ge(y_ready, c + 1)
                sp.dma_start(out_c[c], y_tile(c).rearrange("p (q e) -> p q e", e=E)).then_inc(y_out, 16)
            sp.wait_ge(y_out, 16 * NC)

        @block.gpsimd
        def _(pool):
            pool.memset(ident[:, :], 0.0).then_inc(ident_step, 1)
            pool.wait_ge(ident_step, 1)
            pool.affine_select(out=ident[:, :], in_=ident[:, :], compare_op=ALU.not_equal, fill=1.0, base=0,
                               pattern=[[-1, P]], channel_multiplier=1).then_inc(ident_step, 1)
            pool.wait_ge(ident_step, 2)
            k = 0
            words = [qk_buf[:, s].rearrange("p z a h q -> p z (a h q)").bitcast(F32) for s in range(NBUF)]
            for s in range(NBUF):
                for tile, value in ((words[s][64:SHIFT, :, :], 0.0), (words[s][SHIFT:P, 1, :], TWO_ONES)):
                    if k:
                        pool.wait_ge(rows_const, k)
                    pool.memset(tile, value).then_inc(rows_const, 1)
                    k += 1
            pool.wait_ge(rows_const, k)
            pool.iota(steps_i[:, :], [[1, TILES]], base=0, channel_multiplier=0).then_inc(steps_ready, 1)
            pool.memset(before[:, :], 1.0).then_inc(before_step, 1)
            pool.wait_ge(before_step, 1)
            pool.affine_select(out=before[:, :], in_=before[:, :], compare_op=ALU.is_ge, fill=0.0, base=-1,
                               pattern=[[1, P]], channel_multiplier=-1).then_inc(before_step, 1)

            def split(c, z, m, stored):
                pool.wait_ge(qk_ready[z], c + 1)
                if stored:
                    pool.wait_ge(*stored)
                f, r = qk_f[:, z, c * CH:(c + 1) * CH], rest[:, 1, :]
                for k in range(PARTS):
                    src = f if k == 0 else r
                    if k:
                        pool.wait_ge(split_step[1], 4 * m + 2 * k)
                    ins = pool.tensor_copy(part_of(c)[:, z, k], src)
                    if k == PARTS - 1:
                        ins.then_inc(part_ready[z] if c < 2 else split_late[z], 1)
                    else:
                        ins.then_inc(split_step[1], 1)
                        pool.wait_ge(split_step[1], 4 * m + 2 * k + 1)
                        pool.tensor_tensor(r, src, part_of(c)[:, z, k], ALU.subtract).then_inc(split_step[1], 1)

            for c in range(2):
                split(c, 1, c, None)
            for s in range(2):
                pool.wait_ge(v_ps[s], NC // 2)
            pool.memset(zeros, 0.0).then_inc(zeros_ready, 1)
            pool.wait_ge(zeros_ready, 1)
            pieces = slots_dram.rearrange("(a p c) e -> a p (c e)", p=P, c=8)
            m = 2
            for c in range(2, NC):
                for z in range(2):
                    done = 16 * PARTS * (c - 2)
                    split(c, z, m, (late_stored[z], done) if c > 2 else (first_stored[z], 16 * 2 * PARTS))
                    m += 1
                    pool.wait_ge(split_late[z], c - 1)
                    for k in range(PARTS):
                        pool.dma_start(parts_dram[z][c // 2, :, c % 2, k], part[:, z, k]).then_inc(late_stored[z], 16)
                    if m - 3 < TILES // 8:
                        pool.dma_start(pieces[m - 3], zeros).then_inc(zeros_stored, 16)

            pool.wait_ge(zeros_stored, 16 * (TILES // 8))
            pool.wait_ge(routed, 1)
            for k in range(2):
                for n in range(NT):
                    pool.indirect_dma_start(out=slots_dram, out_offset=bass.IndirectOffsetOnAxis(ap=slot[:, k, n:n + 1], axis=0),
                                            in_=x_all[:, n, :], in_offset=None).then_inc(scattered, 16)
            for s in range(2):
                pool.wait_ge(result_out[s], 16 * TILES // 2)
            pool.wait_ge(scattered, 16 * 2 * NT)
            for k in range(2):
                for n in range(NT):
                    pool.indirect_dma_start(out=picked[k][:, n, :], out_offset=None, in_=results_dram,
                                            in_offset=bass.IndirectOffsetOnAxis(ap=slot[:, k, n:n + 1], axis=0)).then_inc(picked_in, 16)
            pool.wait_ge(picked_in, 16 * 2 * NT)
            pool.wait_ge(gates_ready, 2)
            for k in range(2):
                pool.tensor_tensor(picked[k], picked[k], gm[:, 6, k, :].rearrange("p (n a) -> p n a", a=1)
                                   .broadcast_to([P, NT, E]), ALU.mult).then_inc(mixed_step, 1)
            pool.wait_ge(mixed_step, 2)
            pool.tensor_tensor(picked[0], picked[0], picked[1], ALU.add).then_inc(mixed_step, 1)
            pool.wait_ge(mixed_step, 3)
            pool.tensor_tensor(picked[0], picked[0], bo_row[:, :].rearrange("p (a e) -> p a e", a=1)
                               .broadcast_to([P, NT, E]), ALU.add).then_inc(mixed_step, 1)
            pool.dma_start(picked[1], x_t).then_inc(residual_in, 16)
            pool.wait_ge(residual_in, 16)
            pool.wait_ge(mixed_step, 4)
            pool.tensor_tensor(picked[0], picked[0], picked[1], ALU.add).then_inc(mixed_step, 1)

        @block.scalar
        def _(act):
            act.wait_ge(var_ready, 1)
            act.activation(mom[:, 4, :], mom[:, 3, :], ACT.Sqrt).then_inc(std_ready, 1)
            act.wait_ge(rw_T, 1)
            act.activation(wvr[:, E:E + NE], ps[:, 6, 0:NE], ACT.Copy).then_inc(rw_ready, 1)

            def keep(i, s):
                act.wait_ge(xn_T[s], i + 1)
                act.activation(xnT_st[:, s, :], ps[:, s, :], ACT.Copy).then_inc(xnT_ready[s], 1)
                act.activation(xnT_all[:, bass.ds((2 * i + s) * CH, CH)], ps[:, s, :], ACT.Copy).then_inc(xnT_kept[s], 1)

            def bias(i, s):
                for z in range(2):
                    c = 2 * i + s
                    act.wait_ge(qk_ps[z], c + 1)
                    act.activation(qk_f[:, z, bass.ds(c * CH, CH)], ps[:, 6 + z, :], ACT.Identity, bias=bqk[:, z:z + 1],
                                   scale=SCALE if z == 0 else 1.0).then_inc(qk_ready[z], 1)

            def pair(i):
                for s in range(2):
                    if s == 0:
                        keep(i, 1)
                    elif type(i) is not int or i < NC // 2 - 1:
                        keep(i + 1, 0)
                    act.wait_ge(lg_ready[s], i + 1)
                    for b in range(2):
                        k = s * TPC + 2 * b
                        ins = act.activation(v_all[:, bass.ds(i, 1), :, k:k + 2, :].rearrange("p b g k c -> p (b k) g c"),
                                             v_lg[:, s, b, :, 0:E].rearrange("p k (g c) -> p k g c", g=HG), ACT.Copy)
                    ins.then_inc(v_ready[s], 1)
                    if type(i) is int and i == 0:
                        bias(0, s)
            act.wait_ge(const_step, NE + 5)
            keep(0, 0)
            over_pairs(act, pair)
            with act.Fori(1, NC // 2) as i:
                for s in range(2):
                    bias(i, s)
            act.wait_ge(routed, 1)

            def step(i, c, n):
                for kt in range(KT):
                    u = KT * (6 * i + c) + kt
                    for h in range(HG):
                        act.wait_ge(scores_ready, 4 * u + h + 1)
                        if h == 0 and (n is None or u >= 2):
                            act.wait_ge(pv_done, u - 1)
                        act.activation(probs[:, kt % 2, h], ps[:, score_bank(c, h), :], ACT.Exp).then_inc(exp_done, 1)
                    if kt == 0 and (n is None or n >= 1):
                        evacuate(i, c - 1)

            def evacuate(i, c):
                n = 6 * i + c
                act.wait_ge(pv_done, KT * n + KT)
                act.activation(oT[:, c % 2, :], ps[:, 6, :], ACT.Copy).then_inc(o_out, 1)


            def experts():
                def tile(i, k):
                    s = k % 2
                    act.wait_ge(gu_ready[s], used(i, k) + 1)
                    act.activation(silu[:, s, :], ps[:, s, 0:F], ACT.Silu).then_inc(silu_ready[s], 1)
                    if exists(i, k - 1):
                        turn_hidden(i, k - 1)

                def turn_hidden(i, k):
                    s = k % 2
                    act.wait_ge(hid_T[s], used(i, k) + 1)
                    act.activation(hidT[:, s, :], ps[:, 2 + s, 0:F], ACT.Copy).then_inc(hidT_ready[s], 1)
                over_tiles(act, tile)
                turn_hidden(TILES // 4 - 1, 3)
                act.wait_ge(gexp_in, 1)
                act.activation(gm[:, 2], gm[:, 1], ACT.Exp).then_inc(gexp_out, 1)
            over_halves(act, step, experts)
            evacuate(0, NH - 1)

            for c in range(EARLY, NC):
                act.wait_ge(a_T, c + 1)
                act.activation(attn_T(c), ps[:, 2 + c % 2, :], ACT.Copy).then_inc(a_sb, 1)

        @block.vector
        def _(dve):
            step_no = [0]

            def then(ins):
                step_no[0] += 1
                ins.then_inc(mom_step, 1)
                dve.wait_ge(mom_step, step_no[0])

            dve.memset(ones[:, :], 1.0)
            dve.memset(ones_f[:, :], 1.0)
            dve.memset(rank[:, :], 0.0).then_inc(const_step, 1)
            dve.wait_ge(const_step, 1)
            for e in range(NE):
                dve.memset(rank[:, e:e + 1], float(NE - e)).then_inc(const_step, 1)
            for g in range(NBUF):
                dve.memset(vx[g][:, :, :, D:D + 1], 1.0)
                dve.memset(vx[g][:, :, :, D + 1:32], 0.0).then_inc(vx_const, 1)
            for k in range(4):
                dve.wait_ge(x_in[k], 16)
                for n in range(k * NT // 4, (k + 1) * NT // 4):
                    dve.bn_stats(stats[:, n, :], x_all[:, n, :]).then_inc(stat_done, 1)
            dve.wait_ge(stat_done, NT)
            mean_e, m2_e, mean_o, m2_o = (stats[:, :, k] for k in (1, 2, 4, 5))
            then(dve.tensor_tensor(mom[:, 0, :], mean_e, mean_o, ALU.add))
            then(dve.tensor_scalar(mom[:, 0, :], mom[:, 0, :], 0.5, None, ALU.mult))
            then(dve.tensor_tensor(mom[:, 1, :], mean_e, mean_o, ALU.subtract))
            then(dve.scalar_tensor_tensor(mom[:, 1, :], mom[:, 1, :], 0.25, mom[:, 1, :], ALU.mult, ALU.mult))
            then(dve.tensor_tensor(mom[:, 2, :], m2_e, m2_o, ALU.add))
            then(dve.scalar_tensor_tensor(mom[:, 2, :], mom[:, 2, :], 1.0 / E, mom[:, 1, :], ALU.mult, ALU.add))
            dve.tensor_scalar(mom[:, 3, :], mom[:, 2, :], EPS, None, ALU.add).then_inc(var_ready, 1)
            dve.wait_ge(std_ready, 1)
            then(dve.reciprocal(mom[:, 1, :], mom[:, 4, :]))

            dve.wait_ge(proj_in, 64)
            for z, w in enumerate((wq_in, wk_in)):
                dve.tensor_copy(wqk[:, z, :].rearrange("p (g d h) -> p g d h", g=HG, d=D),
                                w[:, :].rearrange("p (g h d) -> p g d h", g=HG, h=HG)).then_inc(const_step, 1)
            dve.wait_ge(small_in, 16 * 5)
            dve.tensor_copy(b_in[:, 1, :].rearrange("p (g d h) -> p g d h", g=HG, d=D),
                            b_in[:, 0, :].rearrange("p (g h d) -> p g d h", g=HG, h=HG)).then_inc(const_step, 1)
            dve.wait_ge(bias_T, 1)
            dve.tensor_scalar(bqk[:, 0:1], ps[:, 7, 0:1], SCALE, None, ALU.mult)
            dve.tensor_copy(bqk[:, 1:2], ps[:, 7, 1:2]).then_inc(const_step, 1)

            def norm(i, s):
                c = 2 * i + s
                for j in range(TPC):
                    n = c * TPC + j
                    ins = dve.tensor_scalar(xn[:, s, j, :], x_all[:, bass.ds(n, 1), :].rearrange("p a e -> p (a e)"),
                                            mom[:, 0, bass.ds(n, 1)], mom[:, 1, bass.ds(n, 1)],
                                            ALU.subtract, ALU.mult)
                ins.then_inc(xn_ready[s], 1)
                dve.wait_ge(xn_ready[s], i + 1)
                dve.tensor_scalar(x_all[:, bass.ds(c * TPC, TPC), :], xn[:, s], 1.0, None, ALU.mult).then_inc(xn_kept[s], 1)

            def split_q(c):
                dve.wait_ge(qk_ready[0], c + 1)
                f, r = qk_f[:, 0, c * CH:(c + 1) * CH], rest[:, 0, :]
                for k in range(PARTS):
                    src = f if k == 0 else r
                    ins = dve.tensor_copy(part_of(c)[:, 0, k], src)
                    if k == PARTS - 1:
                        ins.then_inc(part_ready[0], 1)
                    else:
                        ins.then_inc(split_step[0], 1)
                        dve.wait_ge(split_step[0], 4 * c + 2 * k + 1)
                        dve.tensor_tensor(r, src, part_of(c)[:, 0, k], ALU.subtract).then_inc(split_step[0], 1)
                        dve.wait_ge(split_step[0], 4 * c + 2 * k + 2)

            def pair(i):
                for s in range(2):
                    if type(i) is not int or i < NC // 2 - 1:
                        dve.wait_ge(xn_T[s], i + 1)
                        norm(i + 1, s)
                    c = 2 * i + s
                    dve.wait_ge(v_ps[s], i + 1)
                    dve.tensor_scalar(lg[:, bass.ds(c * TPC, TPC), :].rearrange("p (b j) e -> p b j e", b=2),
                                      v_lg[:, s, :, :, E:E + NE], 1.0, None, ALU.mult).then_inc(lg_ready[s], 1)
            for s in range(2):
                norm(0, s)
            pair(0)
            for c in range(2):
                split_q(c)
            with dve.Fori(1, NC // 2 - 1) as i:
                pair(i)
            pair(NC // 2 - 1)

            def fill_v(g, s):
                dve.tensor_tensor(vx[s][:, :, :, 0:D],
                                  v_all[:, :, :, :, :].rearrange("p b g k (h d) -> p (b g) k h d", d=D)[:, bass.ds(g, 1)]
                                  .rearrange("p a k h d -> p (a k) h d"),
                                  bv_all[:, :, :].rearrange("p b (g h d) -> p (b g) h d", h=HG, d=D)[:, bass.ds(g, 1)]
                                  .broadcast_to([P, KT, HG, D]), ALU.add).then_inc(vx_ready, 1)

            for s in range(2):
                dve.wait_ge(lg_ready[s], NC // 2)
            dve.wait_ge(const_step, NE + 1)
            rank_bc = rank[:, :].rearrange("p (a e) -> p a e", a=1).broadcast_to([P, NT, NE])

            def bc(v):
                return v.rearrange("p (n a) -> p n a", a=1).broadcast_to([P, NT, NE])

            def largest(logits, k):
                then(dve.tensor_reduce(gm[:, 0, k, :], logits, AX.X, ALU.max))
                then(dve.tensor_tensor(gt[:, 0], logits, bc(gm[:, 0, k, :]), ALU.is_equal))
                then(dve.tensor_tensor(gt[:, 0], gt[:, 0], rank_bc, ALU.mult))
                then(dve.tensor_reduce(gm[:, 7, k, :], gt[:, 0], AX.X, ALU.max))
                then(dve.tensor_tensor(gt[:, 1 + k], rank_bc, bc(gm[:, 7, k, :]), ALU.is_equal))

            largest(lg[:, :, :], 0)
            then(dve.tensor_scalar(gt[:, 3], gt[:, 1], -2.0 * BIG, BIG, ALU.mult, ALU.add))
            then(dve.tensor_tensor(gt[:, 3], gt[:, 3], lg[:, :, :], ALU.min))
            largest(gt[:, 3], 1)
            dve.tensor_tensor(chosen[:, :, :].rearrange("p e n -> p n e"), gt[:, 1], gt[:, 2], ALU.add).then_inc(chosen_ready, 1)
            dve.wait_ge(ranks_ps, 1)
            per_tile = ps[:, 1, 0:NE * NT].rearrange("p (e n) -> p e n", e=NE)
            in_tile = ps[:, 0, 0:NE * NT].rearrange("p (e n) -> p e n", e=NE)
            flat = slot_map[:, 0].rearrange("p e n -> p (e n)")
            then(dve.tensor_copy(slot_map[:, 2], per_tile))
            then(dve.tensor_tensor_scan(flat, ones_f[:, :], slot_map[:, 2].rearrange("p e n -> p (e n)"), 0.0, ALU.mult, ALU.add))
            then(dve.tensor_tensor(slot_map[:, 1], slot_map[:, 0], slot_map[:, 2], ALU.subtract))
            first = slot_map[:, 1, :, 0:1].rearrange("p e n -> p (e n)")
            last = slot_map[:, 0, :, NT - 1:NT].rearrange("p e n -> p (e n)")
            then(dve.tensor_tensor(counts[:, 0, :], last, first, ALU.subtract))
            dve.wait_ge(steps_ready, 1)
            then(dve.tensor_copy(steps[:, :], steps_i[:, :]))
            then(dve.tensor_scalar(counts[:, 1, :], counts[:, 0, :], 1.0 / P, None, ALU.mult))
            then(dve.tensor_tensor(over[:, :, :], counts[:, 1, :].rearrange("p (e a) -> p e a", a=1).broadcast_to([P, NE, NT]),
                                   steps[:, 0:NT].rearrange("p (a n) -> p a n", a=1).broadcast_to([P, NE, NT]), ALU.is_gt))
            then(dve.tensor_reduce(counts[:, 2, :], over[:, :, :], AX.X, ALU.add))
            then(dve.tensor_tensor_scan(counts[:, 3, :], ones_f[:, 0:NE], counts[:, 2, :], 0.0, ALU.mult, ALU.add))
            then(dve.tensor_tensor(counts[:, 4, :], counts[:, 3, :], counts[:, 2, :], ALU.subtract))
            then(dve.scalar_tensor_tensor(counts[:, 5, :], counts[:, 4, :], float(P), first, ALU.mult, ALU.subtract))
            then(dve.tensor_tensor(slot_map[:, 1], slot_map[:, 1],
                                   counts[:, 5, :].rearrange("p (e a) -> p e a", a=1).broadcast_to([P, NE, NT]), ALU.add))
            then(dve.tensor_tensor(slot_map[:, 1], slot_map[:, 1], in_tile, ALU.add))
            for k in range(2):
                then(dve.tensor_tensor(gt[:, 3], gt[:, 1 + k], slot_map[:, 1].rearrange("p e n -> p n e"), ALU.mult))
                then(dve.tensor_reduce(slot_f[:, k, :], gt[:, 3], AX.X, ALU.add))
            then(dve.tensor_copy(slot[:, :, :], slot_f[:, :, :]))
            then(dve.tensor_tensor(tile_e[:, :, 0:NE - 1],
                                   counts[:, 3, 0:NE - 1].rearrange("p (a e) -> p a e", a=1).broadcast_to([P, TILES, NE - 1]),
                                   steps[:, :].rearrange("p (t a) -> p t a", a=1).broadcast_to([P, TILES, NE - 1]), ALU.is_le))
            then(dve.tensor_reduce(tile_f[:, :], tile_e[:, :, 0:NE - 1], AX.X, ALU.add))
            dve.tensor_copy(tile_expert[:, :], tile_f[:, :]).then_inc(routed, 1)

            def maxima(i, c, r, reused=True):
                n = 6 * i + c
                if r == 0 and reused:
                    dve.wait_ge(m_T, n - 1)
                dve.wait_ge(x_ready, 16 * n + r + 1)
                dve.tensor_reduce(mneg[:, c % 2, r:r + 1], ps[:, 2 + 2 * (r % 2):4 + 2 * (r % 2), :], AX.XY, ALU.max,
                                  negate=True).then_inc(max_done, 1)

            def split_max(i, c, reused):
                n, k = 6 * i + c, c % 2
                src = ps[0:HG * TPC, 7, 0:P]
                dve.wait_ge(m_T, n + 1)
                if reused:
                    dve.wait_ge(m_stored, 16 * n - 16)
                dve.tensor_copy(m_parts[:, k, 0], src).then_inc(m_hi, 1)
                dve.wait_ge(m_hi, n + 1)
                dve.tensor_tensor(m_rest[:, 0], src, m_parts[:, k, 0], ALU.subtract).then_inc(m_read, 1)
                dve.wait_ge(m_read, n + 1)
                dve.tensor_copy(m_parts[:, k, 1], m_rest[:, 0]).then_inc(m_mid, 1)
                dve.wait_ge(m_mid, n + 1)
                dve.tensor_tensor(m_rest[:, 1], m_rest[:, 0], m_parts[:, k, 1], ALU.subtract).then_inc(m_rest2, 1)
                dve.wait_ge(m_rest2, n + 1)
                dve.tensor_copy(m_parts[:, k, 2], m_rest[:, 1]).then_inc(m_split, 1)

            def divide(i, c):
                n = 6 * i + c
                o = ps[:, 7, :].rearrange("p (a c) -> p a c", c=32)
                dve.wait_ge(o_T, n + 1)
                dve.reciprocal(recip[:, c % 2, :], o[:, :, D:D + 1].rearrange("p a c -> p (a c)")).then_inc(recip_ready, 1)
                dve.wait_ge(recip_ready, n + 1)
                dve.tensor_tensor(attn_all[:, bass.ds(n, 1), :, :].rearrange("p n q (h d) -> p (n q h) d", d=D),
                                  o[:, :, 0:D],
                                  recip[:, c % 2, :].rearrange("p (a c) -> p a c", c=1).broadcast_to([P, HG * TPC, D]),
                                  ALU.mult).then_inc(attn_ready, 1)

            for r in range(2 * KT):
                maxima(0, 0, r, False)
            for r in range(AHEAD):
                maxima(0, 1, r, False)
                if r == 1:
                    split_max(0, 0, False)
            for s in range(2):
                dve.wait_ge(v_ready[s], NC // 2)
            for g in range(NBUF):
                fill_v(g, g)

            def stage(c):
                if c == 0:
                    dve.wait_ge(scores_ready, 4 * KT * (NH - 2))
                if c >= 2:
                    dve.wait_ge(a_T, c - 1)
                dve.wait_ge(attn_ready, (c // 2 * HG + HG - 1) * 2 + c % 2 + 1)
                for q in range(TPC):
                    ins = dve.tensor_copy(staged_tile(c)[:, q * E:(q + 1) * E].rearrange("p (g c) -> p g c", g=HG),
                                          qk_f[:, 0, :].rearrange("p (b g a q c) -> p b a q g c", b=B, g=HG, a=2, q=TPC)
                                          [:, c // 2, c % 2, q])
                ins.then_inc(a_staged, 1)

            def keep_turned(c):
                dve.wait_ge(a_T, c + 1)
                dve.tensor_copy(attn_T(c), ps[:, 2 + c % 2, :]).then_inc(a_sb, 1)

            def finish(c):
                dve.wait_ge(a_proj, c + 1)
                dve.tensor_tensor(y_tile(c).rearrange("p (q e) -> p q e", e=E),
                                  ps[:, 4 + c % 2, :].rearrange("p (q e) -> p q e", e=E),
                                  x_all[:, c * TPC:(c + 1) * TPC, :], ALU.add).then_inc(y_ready, 1)

            def step(i, c, n):
                if n is None and c == 4:
                    dve.wait_ge(split_late[0], NC - 2)
                for kt in range(KT):
                    for r in (2 * kt, 2 * kt + 1):
                        if n == 0:
                            for c2, r2 in FIRST_MAXIMA[r]:
                                maxima(0, c2, r2, c2 == 2)
                        elif n is None or n + 2 < NH:
                            maxima(i, c + 2, r)
                    if kt == 1 and c % 2 == 0 and c >= 2 and (n is None or n + 4 < NH):
                        dve.wait_ge(pv_done, 2 * KT * group(i, c))
                        fill_v(group(i, c + 4), buf(c + 4))
                    if n == NH - 2:
                        if kt < EARLY:
                            stage(kt)
                        if 1 <= kt <= EARLY:
                            keep_turned(kt - 1)
                    if kt == (4 if n == 0 else 3) and (n is None or n + 1 < NH):
                        split_max(i, c + 1, n is None or n >= 1)
                    if kt == 6 and (n is None or n >= 1):
                        divide(i, c - 1)

            def experts():
                def tile(i, k):
                    s = k % 2
                    if exists(i, k + 2):
                        take(i, k + 2)
                    dve.wait_ge(silu_ready[s], used(i, k) + 1)
                    dve.tensor_tensor(hid[:, s, :], silu[:, s, :], ps[:, s, F:2 * F], ALU.mult).then_inc(hid_ready[s], 1)
                    if exists(i, k - 2):
                        give(i, k - 2)

                def take(i, k):
                    s = k % 2
                    dve.wait_ge(xg_T[k % 4], used(i, k, 4) + 1)
                    dve.tensor_copy(xgT[:, s, :], ps[:, 7, 0:P]).then_inc(xgT_ready[s], 1)

                def give(i, k):
                    s = k % 2
                    dve.wait_ge(down_done[s], used(i, k) + 1)
                    past(dve, result_out[s], used(i, k), 16)
                    dve.tensor_copy(result[:, s, :], ps[:, 4 + s, 0:E]).then_inc(result_ready[s], 1)
                take(0, 0)
                take(0, 1)
                over_tiles(dve, tile)
                give(TILES // 4 - 1, 2)
                give(TILES // 4 - 1, 3)
                dve.tensor_scalar(gm[:, 1], gm[:, 0], -1.0, 88.0, ALU.mult, ALU.min).then_inc(gexp_in, 1)
                dve.wait_ge(gexp_out, 1)
                then(dve.tensor_scalar(gm[:, 3], gm[:, 2], 1.0, None, ALU.add))
                then(dve.reciprocal(gm[:, 4], gm[:, 3]))
                then(dve.tensor_tensor(gm[:, 5, 0, :], gm[:, 4, 0, :], gm[:, 4, 1, :], ALU.add))
                then(dve.tensor_scalar(gm[:, 5, 0, :], gm[:, 5, 0, :], 1e-10, None, ALU.add))
                then(dve.reciprocal(gm[:, 5, 1, :], gm[:, 5, 0, :]))
                for k in range(2):
                    dve.tensor_tensor(gm[:, 6, k, :], gm[:, 4, k, :], gm[:, 5, 1, :], ALU.mult).then_inc(gates_ready, 1)
            over_halves(dve, step, experts)
            dve.wait_ge(mixed_step, 5)
            for c in range(4):
                finish(c)
            divide(0, NH - 1)
            for c in range(EARLY, NC):
                stage(c)
            for c in range(4, NC):
                finish(c)

        @block.tensor
        def _(pe):
            pe.wait_ge(ident_step, 2)
            pe.wait_ge(small_in, 16 * 5)
            pe.transpose(ps[:, 6, 0:NE], rw_in[:, :], ident[0:NE, 0:NE]).then_inc(rw_T, 1)
            pe.wait_ge(const_step, NE + 4)
            pe.transpose(ps[:, 7, 0:2], b_in[:, 1, :], ident[0:2, 0:2]).then_inc(bias_T, 1)
            pe.wait_ge(rw_ready, 1)
            pe.wait_ge(proj_in, 64)

            def turn_norm(i, s):
                pe.wait_ge(xn_ready[s], i + 1)
                past(pe, xnT_kept[s], i)
                for j in range(TPC):
                    mm = pe.transpose(ps[:, s, j * P:(j + 1) * P], xn[:, s, j, :], ident[:, :])
                mm.then_inc(xn_T[s], 1)

            def project(i, s, xnT):
                for z in range(2):
                    past(pe, qk_ready[z], 2 * i + s)
                    pe.matmul(ps[:, 6 + z, :], wqk[:, z, :], xnT, start=True, stop=True).then_inc(qk_ps[z], 1)

            def pair(i):
                for s in range(2):
                    if s == 0:
                        turn_norm(i, 1)
                    elif type(i) is not int or i < NC // 2 - 1:
                        turn_norm(i + 1, 0)
                    pe.wait_ge(xnT_ready[s], i + 1)
                    past(pe, lg_ready[s], i)
                    past(pe, v_ready[s], i)
                    for j in range(TPC):
                        mm = pe.matmul(v_lg[:, s, j // 2, j % 2], xnT_st[:, s, j * P:(j + 1) * P], wvr[:, :],
                                       start=True, stop=True)
                    mm.then_inc(v_ps[s], 1)
                    if type(i) is int and i == 0:
                        if s == 0:
                            pe.wait_ge(const_step, NE + 5)
                        project(0, s, xnT_st[:, s, :])
            turn_norm(0, 0)
            over_pairs(pe, pair)
            for s in range(2):
                pe.wait_ge(xnT_kept[s], NC // 2)
            with pe.Fori(1, NC // 2 - 1) as i:
                for s in range(2):
                    project(i, s, xnT_all[:, bass.ds((2 * i + s) * CH, CH)])
            pe.wait_ge(chosen_ready, 1)
            pe.wait_ge(before_step, 2)
            pe.matmul(ps[:, 0, 0:NE * NT], before[:, :], chosen[:, :, :].rearrange("p e n -> p (e n)"), start=True, stop=True)
            pe.matmul(ps[:, 1, 0:NE * NT], ones[:, :], chosen[:, :, :].rearrange("p e n -> p (e n)"),
                      start=True, stop=True).then_inc(ranks_ps, 1)
            for s in range(2):
                project(NC // 2 - 1, s, xnT_all[:, (NC - 2 + s) * CH:(NC - 1 + s) * CH])

            for s in range(2):
                pe.wait_ge(v_ready[s], NC // 2)
            pe.wait_ge(rows_const, 2 * NBUF)
            pe.wait_ge(vx_const, NBUF)

            def maxima_of(i, c, r, n):
                if n == 0:
                    for c2, r2 in FIRST_MAXIMA[r]:
                        maxima(0, c2, r2)
                elif n is None or n + 2 < NH:
                    maxima(i, c + 2, r)

            def maxima(i, c, r):
                n, s = 6 * i + c, buf(c)
                if r == 0 and c % 2 == 0:
                    pe.wait_ge(qk_in[s], LOADS * (turn(i, c) + 1))
                h, q = r // TPC, r % TPC
                if c >= 1 or r >= 2:
                    pe.wait_ge(max_done, 16 * n + r - 1)
                for half in range(2):
                    mm = pe.matmul(ps[:, 2 + 2 * (r % 2) + half, :], q_sb[s][0:KX, c % 2, h, q * P:(q + 1) * P],
                                   k_sb[s][0:KX, half, h, :], start=True, stop=True)
                mm.then_inc(x_ready, 1)

            def turn_max(i, c, first):
                n = 6 * i + c
                pe.wait_ge(max_done, 16 * n + 16)
                if not first:
                    pe.wait_ge(attn_ready, n - 2)
                pe.transpose(ps[0:HG * TPC, 7, 0:P], mneg[:, c % 2, :], ident[:, :]).then_inc(m_T, 1)

            def turn_output(i, c):
                n = 6 * i + c
                pe.wait_ge(o_out, n + 1)
                if type(n) is int and n >= NH - 2:
                    pe.wait_ge(attn_ready, n)
                else:
                    pe.wait_ge(m_read, n + 3)
                for q in range(TPC):
                    mm = pe.transpose(ps[:, 7, q * P:(q + 1) * P], oT[:, c % 2, q * P:(q + 1) * P], ident[:, :])
                mm.then_inc(o_T, 1)

            def scores(i, c, kt, h, first):
                n, s = 6 * i + c, buf(c)
                if kt == 0 and h == 0:
                    pe.wait_ge(m_in, 16 * n + 16)
                if h == 2 and kt == 0 and c == NH - 2:
                    pe.wait_ge(max_done, 16 * NH)
                if h == 2 and kt == 0 and c == NH - 1:
                    pe.wait_ge(a_sb, EARLY)
                if c >= NH - 2 and kt >= 1:
                    pe.wait_ge(exp_done, 4 * (KT * n + kt) + h - 3)
                elif not first:
                    pe.wait_ge(exp_done, 4 * (KT * n + kt) + h - 1)
                pe.matmul(ps[:, score_bank(c, h), :], k_sb[s][0:KS, kt // 4, h, kt % 4 * P:(kt % 4 + 1) * P],
                          q_sb[s][0:KS, c % 2, h, :], start=True, stop=True).then_inc(scores_ready, 1)

            def weigh(i, c, kt, half):
                n, s = 6 * i + c, buf(c)
                if half == 0:
                    pe.wait_ge(exp_done, 4 * (KT * n + kt) + 4)
                if kt == 0 and half == 0:
                    if c >= 1:
                        pe.wait_ge(o_out, n)
                    if c % 2 == 0:
                        pe.wait_ge(vx_ready, group(i, c) + 1)
                for h in range(HG):
                    mm = pe.matmul(ps[32 * h:32 * h + 32, 6, half * CH // 2:(half + 1) * CH // 2], vx[s][:, kt, h, :],
                                   probs[:, kt % 2, h, half * CH // 2:(half + 1) * CH // 2],
                                   start=(kt == 0 and half == 0), stop=(kt == KT - 1 and half == 1))
                if half == 1:
                    mm.then_inc(pv_done, 1)

            for r in range(2 * KT):
                maxima(0, 0, r)
            for r in range(AHEAD):
                maxima(0, 1, r)
                if r == 1:
                    for z in range(2):
                        pe.wait_ge(qk_ready[z], NC)
                    turn_max(0, 0, True)
            pe.wait_ge(routed, 1)

            def weigh_before(i, c, kt, half, n):
                if kt >= 1:
                    weigh(i, c, kt - 1, half)
                elif n is None or n >= 1:
                    weigh(i, c - 1, KT - 1, half)

            def turn_attn(c):
                pe.wait_ge(a_staged, c + 1)
                if c == 0:
                    pe.wait_ge(max_done, 16 * NH)
                if c >= 2:
                    pe.wait_ge(a_sb, c - 1)
                for q in range(TPC):
                    mm = pe.transpose(ps[:, 2 + c % 2, q * P:(q + 1) * P], staged_tile(c)[:, q * P:(q + 1) * P], ident[:, :])
                mm.then_inc(a_T, 1)

            def project_attn(c):
                pe.wait_ge(a_sb, c + 1)
                if c >= 2:
                    pe.wait_ge(y_ready, c - 1)
                for q in range(TPC):
                    mm = pe.matmul(ps[:, 4 + c % 2, q * E:(q + 1) * E], attn_T(c)[:, q * P:(q + 1) * P], wo[:, :],
                                   start=True, stop=True)
                mm.then_inc(a_proj, 1)

            def step(i, c, n):
                for kt in range(KT):
                    scores(i, c, kt, 0, n == 0 and kt == 0)
                    maxima_of(i, c, 2 * kt, n)
                    scores(i, c, kt, 1, n == 0 and kt == 0)
                    weigh_before(i, c, kt, 0, n)
                    scores(i, c, kt, 2, False)
                    maxima_of(i, c, 2 * kt + 1, n)
                    scores(i, c, kt, 3, False)
                    weigh_before(i, c, kt, 1, n)
                    if n == NH - 2 and 1 <= kt <= EARLY:
                        turn_attn(kt - 1)
                    if n == NH - 1 and kt >= KT - 2:
                        project_attn(kt - KT + 2)
                    if kt == (3 if n == 0 else 2) and (n is None or n + 1 < NH):
                        turn_max(i, c + 1, n is not None and n < 2)
                    if kt == 5 and (n is None or n >= 1):
                        turn_output(i, c - 1)

            def experts():
                pe.wait_ge(ffn_in, 16 * (2 * NE + 1))
                pe.wait_ge(exp_done, 4 * KT * BREAK)
                pe.wait_ge(max_done, 16 * (BREAK + 2))
                pe.wait_ge(attn_ready, BREAK - 1)
                pe.wait_ge(m_read, BREAK + 1)

                def expert(i, k):
                    return nc.values_load(tile_expert[0:1, bass.ds(4 * i + k, 1)], engines=[mybir.EngineType.PE],
                                          min_val=0, max_val=NE - 1,
                                          skip_runtime_bounds_check_because="it counts how many of seven ends are passed")

                def take(i, k):
                    pe.wait_ge(xg_in[k % 4], 16 * (used(i, k, 4) + 1))
                    if exists(i, k - 1):
                        pe.wait_ge(xgT_ready[(k - 1) % 2], used(i, k - 1) + 1)
                    pe.transpose(ps[:, 7, 0:P], xg[:, k % 4, :], ident[:, :]).then_inc(xg_T[k % 4], 1)

                def turn_hidden(i, k):
                    s = k % 2
                    pe.wait_ge(hid_ready[s], used(i, k) + 1)
                    for f in range(F // P):
                        mm = pe.transpose(ps[:, 2 + s, f * P:(f + 1) * P], hid[:, s, f * P:(f + 1) * P], ident[:, :])
                    mm.then_inc(hid_T[s], 1)

                def down(i, k):
                    s, e = k % 2, expert(i, k)
                    pe.wait_ge(hidT_ready[s], used(i, k) + 1)
                    for f in range(F // P):
                        mm = pe.matmul(ps[:, 4 + s, 0:E], hidT[:, s, f * P:(f + 1) * P],
                                       w_dn[:, bass.ds(e, 1), f].rearrange("p e d -> p (e d)"),
                                       start=(f == 0), stop=(f == F // P - 1))
                    mm.then_inc(down_done[s], 1)

                def tile(i, k):
                    s, e = k % 2, expert(i, k)
                    pe.wait_ge(xgT_ready[s], used(i, k) + 1)
                    pe.matmul(ps[:, s, :], xgT[:, s, :], w_gu[:, bass.ds(e, 1)].rearrange("p e a f -> p (e a f)"),
                              start=True, stop=True).then_inc(gu_ready[s], 1)
                    if exists(i, k + 2):
                        take(i, k + 2)
                    if exists(i, k - 1):
                        turn_hidden(i, k - 1)
                    if exists(i, k - 2):
                        down(i, k - 2)
                take(0, 0)
                take(0, 1)
                over_tiles(pe, tile)
                turn_hidden(TILES // 4 - 1, 3)
                down(TILES // 4 - 1, 2)
                pe.wait_ge(result_ready[1], TILES // 2 - 1)
                down(TILES // 4 - 1, 3)
                for s in range(2):
                    pe.wait_ge(result_ready[s], TILES // 2)
            over_halves(pe, step, experts)
            weigh(0, NH - 1, KT - 1, 0)
            weigh(0, NH - 1, KT - 1, 1)
            for c in range(2, 4):
                project_attn(c)
            turn_output(0, NH - 1)
            for c in range(4, EARLY):
                project_attn(c)
            for c in range(EARLY, NC):
                turn_attn(c)
            for c in range(EARLY, NC):
                project_attn(c)


_INS = ["L0_attn_inputs", "L0_attn_Wq", "L0_attn_bq", "L0_attn_Wk", "L0_attn_bk", "L0_attn_Wv", "L0_attn_bv",
        "L0_attn_Wo", "L0_attn_bo", "L0_ffn_router_w", "L0_ffn_w_gate", "L0_ffn_w_up", "L0_ffn_w_down"]


def kernel(**inputs):
    import concourse.bacc as bacc
    from concourse.bass_utils import run_bass_kernel_spmd

    nc = bacc.Bacc("TRN2", target_bir_lowering=False, num_devices=1)
    arrays, args = {}, []
    for name in _INS:
        a = np.ascontiguousarray(inputs[name])
        arrays[name] = a
        args.append(nc.dram_tensor(name, a.shape, mybir.dt.from_np(a.dtype), kind="ExternalInput").ap())
    y = nc.dram_tensor("y", (B, S, E), F32, kind="ExternalOutput").ap()
    build(nc, *args, y)
    return run_bass_kernel_spmd(nc, [arrays], core_ids=[0]).results[0]["y"]
```
